# Optimizing a Trainium2 kernel written in Bass

```python
import numpy as np
import jax
import jax.numpy as jnp

def _softmax(x, axis=-1):
    return jax.nn.softmax(x, axis=axis)

def _gelu(x):
    return jax.nn.gelu(x, approximate=True)

def _silu(x):
    return jax.nn.silu(x)

def _sigmoid(x):
    return jax.nn.sigmoid(x)

def _layernorm(x, axis=-1, eps=1e-05):
    m = jnp.mean(x, axis=axis, keepdims=True)
    v = jnp.var(x, axis=axis, keepdims=True)
    return (x - m) / jnp.sqrt(v + eps)

def _scatter_add(tgt, idx, src, axis=0):
    return tgt.at[idx].add(src)

def _segment_sum(src, seg, n):
    return jax.ops.segment_sum(src, seg, n)
kernel_name = 'mk_conv_seq_d2_conv_nchw64_r2_0475f8'

def setup_inputs(seed: int=0):
    np.random.seed(seed)
    _w = jnp.asarray

    def _rec_inputs():
        import jax
        import jax.numpy as jnp
        _gk = jax.random.key(seed)
        x = 7.22e-05 + 1 * jax.random.normal(jax.random.fold_in(_gk, 1), (8, 32, 64, 64), jnp.float32)
        return x
    x = _rec_inputs()

    def _L0_conv_setup():
        import jax, jax.numpy as jnp
        import numpy as np
        K = 3
        PAD = K // 2
        CENTER = K * K // 2

        def _conv(x, w, b, pad):
            y = jax.lax.conv_general_dilated(x, w, window_strides=(1, 1), padding=[(pad, pad), (pad, pad)], dimension_numbers=('NCHW', 'OIHW', 'NCHW'))
            return y + b[None, :, None, None]
        key = jax.random.key(seed)
        k1, k2, k3 = jax.random.split(key, 3)
        B, C, H, W = (8, 32, 64, 64)
        x = jax.random.normal(k1, (B, C, H, W), dtype=jnp.float32)
        w1 = jax.random.normal(k2, (C // 2, C, 3, 3), dtype=jnp.float32) * 0.05
        b1 = jnp.zeros((C // 2,), dtype=jnp.float32)
        w2 = jax.random.normal(k3, (K * K, C // 2, 1, 1), dtype=jnp.float32) * 0.05
        b2 = jnp.zeros((K * K,), dtype=jnp.float32)
        return {'x': x, 'w1': w1, 'b1': b1, 'w2': w2, 'b2': b2}
    _L0_conv_all = _L0_conv_setup()
    _L0_conv_in = {k: v for k, v in _L0_conv_all.items() if k in ('w1', 'b1', 'w2', 'b2')}
    del _L0_conv_all

    def _L1_conv_setup():
        import jax, jax.numpy as jnp
        import numpy as np
        H_STEP = 0.1
        DEPTH = 4
        BN_EPS = 1e-05

        def project(K):
            return K - K.mean(axis=(-2, -1), keepdims=True)

        def conv3x3(x, K):
            return jax.lax.conv_general_dilated(x, K, window_strides=(1, 1), padding=[(1, 1), (1, 1)], dimension_numbers=('NCHW', 'OIHW', 'NCHW'))

        def conv3x3T(x, K):
            Kt = jnp.flip(jnp.transpose(K, (1, 0, 2, 3)), axis=(-2, -1))
            return conv3x3(x, Kt)

        def batchnorm(x, gamma, beta):
            mean = x.mean(axis=(0, 2, 3), keepdims=True)
            var = ((x - mean) ** 2).mean(axis=(0, 2, 3), keepdims=True)
            xn = (x - mean) * jax.lax.rsqrt(var + BN_EPS)
            return gamma[None, :, None, None] * xn + beta[None, :, None, None]

        def diag_imp_conv_fft(x, B, h):
            C, _, kH, kW = B.shape
            Himg, Wimg = (x.shape[-2], x.shape[-1])
            Bp = jnp.zeros((C, Himg, Wimg), dtype=x.dtype).at[:, :kH, :kW].set(B[:, 0])
            Bp = jnp.roll(Bp, shift=(-(kH // 2), -(kW // 2)), axis=(-2, -1))
            Bh = jnp.fft.fft2(Bp)
            t = 1.0 / (h * (Bh.real ** 2 + Bh.imag ** 2) + 1.0)
            xh = jnp.fft.fft2(x)
            return jnp.real(jnp.fft.ifft2(xh * t[None])).astype(x.dtype)
        key = jax.random.key(seed)
        ks = jax.random.split(key, 3)
        x = jax.random.normal(ks[0], (32, 32, 64, 64), dtype=jnp.float32)
        K = jax.random.normal(ks[1], (DEPTH, 32, 32, 3, 3), dtype=jnp.float32) * 0.001
        L = jax.random.normal(ks[2], (DEPTH, 32, 1, 3, 3), dtype=jnp.float32)
        gamma = jnp.ones((DEPTH, 32), dtype=jnp.float32)
        beta = jnp.zeros((DEPTH, 32), dtype=jnp.float32)
        return {'x': x, 'K': K, 'L': L, 'gamma': gamma, 'beta': beta}
    _L1_conv_all = _L1_conv_setup()
    _L1_conv_in = {k: v for k, v in _L1_conv_all.items() if k in ('K', 'L', 'gamma', 'beta')}
    del _L1_conv_all
    return {'x': x, 'L0_conv_w1': _L0_conv_in['w1'], 'L0_conv_b1': _L0_conv_in['b1'], 'L0_conv_w2': _L0_conv_in['w2'], 'L0_conv_b2': _L0_conv_in['b2'], 'L1_conv_K': _L1_conv_in['K'], 'L1_conv_L': _L1_conv_in['L'], 'L1_conv_gamma': _L1_conv_in['gamma'], 'L1_conv_beta': _L1_conv_in['beta']}

def reference(x, L0_conv_w1, L0_conv_b1, L0_conv_w2, L0_conv_b2, L1_conv_K, L1_conv_L, L1_conv_gamma, L1_conv_beta):
    import jax
    import jax.numpy as jnp

    def _L0_conv_ref(x, w1, b1, w2, b2):
        import jax, jax.numpy as jnp
        import numpy as np
        K = 3
        PAD = K // 2
        CENTER = K * K // 2

        def _conv(x, w, b, pad):
            y = jax.lax.conv_general_dilated(x, w, window_strides=(1, 1), padding=[(pad, pad), (pad, pad)], dimension_numbers=('NCHW', 'OIHW', 'NCHW'))
            return y + b[None, :, None, None]
        B, C, H, W = x.shape
        h = _conv(x, w1, b1, pad=1)
        h = jnp.where(h >= 0, h, 0.2 * h)
        w_lp = jax.nn.softmax(_conv(h, w2, b2, pad=0), axis=1)
        delta = jnp.zeros_like(w_lp).at[:, CENTER].set(1.0)
        w_hp = delta - w_lp
        xp = jnp.pad(x, ((0, 0), (0, 0), (PAD, PAD), (PAD, PAD)))
        high = jnp.zeros_like(x)
        for i in range(K):
            for j in range(K):
                k = i * K + j
                high = high + xp[:, :, i:i + H, j:j + W] * w_hp[:, k:k + 1]
        return x + high

    def _L1_conv_ref(x, K, L, gamma, beta):
        import jax, jax.numpy as jnp
        import numpy as np
        H_STEP = 0.1
        DEPTH = 4
        BN_EPS = 1e-05

        def project(K):
            return K - K.mean(axis=(-2, -1), keepdims=True)

        def conv3x3(x, K):
            return jax.lax.conv_general_dilated(x, K, window_strides=(1, 1), padding=[(1, 1), (1, 1)], dimension_numbers=('NCHW', 'OIHW', 'NCHW'))

        def conv3x3T(x, K):
            Kt = jnp.flip(jnp.transpose(K, (1, 0, 2, 3)), axis=(-2, -1))
            return conv3x3(x, Kt)

        def batchnorm(x, gamma, beta):
            mean = x.mean(axis=(0, 2, 3), keepdims=True)
            var = ((x - mean) ** 2).mean(axis=(0, 2, 3), keepdims=True)
            xn = (x - mean) * jax.lax.rsqrt(var + BN_EPS)
            return gamma[None, :, None, None] * xn + beta[None, :, None, None]

        def diag_imp_conv_fft(x, B, h):
            C, _, kH, kW = B.shape
            Himg, Wimg = (x.shape[-2], x.shape[-1])
            Bp = jnp.zeros((C, Himg, Wimg), dtype=x.dtype).at[:, :kH, :kW].set(B[:, 0])
            Bp = jnp.roll(Bp, shift=(-(kH // 2), -(kW // 2)), axis=(-2, -1))
            Bh = jnp.fft.fft2(Bp)
            t = 1.0 / (h * (Bh.real ** 2 + Bh.imag ** 2) + 1.0)
            xh = jnp.fft.fft2(x)
            return jnp.real(jnp.fft.ifft2(xh * t[None])).astype(x.dtype)
        h = H_STEP
        for j in range(K.shape[0]):
            Kj = project(K[j])
            Lj = project(L[j])
            z = conv3x3(x, Kj)
            z = batchnorm(z, gamma[j], beta[j])
            z = jax.nn.relu(z)
            z = conv3x3T(z, Kj)
            x = x + h * z
            x = batchnorm(x, gamma[j], beta[j])
            x = diag_imp_conv_fft(x, Lj, h)
        return x

    def _gn(v, G=32, eps=1e-05):
        B_, C_, H_, W_ = v.shape
        g = v.reshape(B_, G, C_ // G, H_, W_)
        m = jnp.mean(g, axis=(2, 3, 4), keepdims=True)
        s = jnp.var(g, axis=(2, 3, 4), keepdims=True)
        return ((g - m) / jnp.sqrt(s + eps)).reshape(v.shape)

    def _ln_c(v, eps=1e-06):
        m = jnp.mean(v, axis=1, keepdims=True)
        s = jnp.var(v, axis=1, keepdims=True)
        return (v - m) / jnp.sqrt(s + eps)

    def _ln_t(v, eps=1e-05):
        m = jnp.mean(v, axis=-1, keepdims=True)
        s = jnp.var(v, axis=-1, keepdims=True)
        return (v - m) / jnp.sqrt(s + eps)

    def _to_tokens(v):
        B_, C_, H_, W_ = v.shape
        return v.reshape(B_, C_, H_ * W_).transpose(0, 2, 1)

    def _from_tokens(t, like):
        B_, C_, H_, W_ = like.shape
        return t.transpose(0, 2, 1).reshape(B_, C_, H_, W_)
    x = _L0_conv_ref(x, L0_conv_w1, L0_conv_b1, L0_conv_w2, L0_conv_b2)
    x = _L1_conv_ref(x, L1_conv_K, L1_conv_L, L1_conv_gamma, L1_conv_beta)
    return x

_drawn_inputs = setup_inputs


def setup_inputs(seed=0):
    import zlib

    import numpy as np

    out = dict(_drawn_inputs(seed))
    spreads = {'L0_conv_b1': (0.0, 2.0),
     'L0_conv_b2': (0.0, 0.412),
     'L1_conv_gamma': (1.0, 0.2),
     'L1_conv_beta': (0.0, 0.1)}
    factors = {'L1_conv_K': 22.264, 'L0_conv_w1': 2.785}
    for name, (base, spread) in spreads.items():
        noise = np.random.default_rng([zlib.crc32(name.encode()), seed]).standard_normal(out[name].shape)
        drawn = base * np.exp(spread * noise) if base else spread * noise
        out[name] = jnp.asarray(drawn.astype(out[name].dtype))
    for name, factor in factors.items():
        out[name] = (out[name] * factor).astype(out[name].dtype)
    return out
```

```python
import numpy as np
import concourse.bass as bass
from concourse import mybir
from contextlib import ExitStack

B, C, H, W = 8, 32, 64, 64
R = 128 // C
G = H // R
BP = B // 2
TAPS = 9
SUM_AT = 3
HID = C // 2
DEPTH = 4
STEP = 0.1
BN_EPS = 1e-5
LEAK = 0.2

ROW = 2 * W
GROUP = ROW + 2
REG = G * GROUP + 4
REG2 = (G + 1) * GROUP + 4
CH = 4
Q = G // CH
NCH = BP * Q
N = CH * ROW
BANKS = 8
WORK = 2048

C_ID, C_FW, C_FH, C_IR, C_IW, C_AVG, C_ERE, C_EIM = (128 * i for i in range(8))
C_CS = 8 * 128
C_ONE = C_CS + 64
C_SGN = C_ONE + 1
C_MASK = C_SGN + 1
C_ALL = C_MASK + 2
P_K = 0
P_F = P_K + 2 * TAPS * C
P_GB = P_F + 2 * 2 * 3 * C
P_L = P_GB + 2
P_L9 = P_L + (C // 2) * 3
P_ALL = P_L9 + (C // 2) * TAPS


def prologue_schedule():
    order = [("conv", 0, q) for q in range(Q)] + [("logits", 0, i) for i in range(2)] + [("probsT", 0, q) for q in range(Q)]
    for bp in range(BP):
        if bp + 1 < BP:
            order += [("conv", bp + 1, q) for q in range(Q)] + [("logits", bp + 1, i) for i in range(2)]
        for q in range(Q):
            order += [("spread", bp, q, k) for k in range(SUM_AT)]
            if bp * Q + q > 0:
                order.append(("sum", bp * Q + q - 1))
            order += [("spread", bp, q, k) for k in range(SUM_AT, TAPS)]
        if bp + 1 < BP:
            order += [("probsT", bp + 1, q) for q in range(Q)]
    order.append(("sum", NCH - 1))
    return order


def layer_schedule():
    order = [("conv1", c) for c in range(NCH)]
    order += [("table", 0), ("mean", 1), ("table", 1), ("var", 1), ("table", 2), ("table", 3)]
    order += [("conv2", c) for c in range(NCH)]
    for k in range(BP + 4):
        for stage, lag in (("invW", 4), ("invH", 3), ("fwdH", 2), ("fwdW", 1), ("turn", 0)):
            if 0 <= k - lag < BP:
                order += [(stage, (k - lag) * Q + q) for q in range(Q)]
        if k == 1:
            order.append(("mean", 2))
        if k == 2:
            order.append(("var", 2))
    return order


PRO = {step: n for n, step in enumerate(prologue_schedule())}
LAY = {step: n for n, step in enumerate(layer_schedule())}
PRO_ROUNDS = len(PRO) // BANKS
LAY_ROUNDS = len(LAY) // BANKS
assert PRO_ROUNDS * BANKS == len(PRO) and LAY_ROUNDS * BANKS == len(LAY)
PRO_LINKS, LAY_LINKS = 41, 27


def build(nc, x_in, par, w1, b1, w2, cst, sel, idb, out):
    f32, bf16 = mybir.dt.float32, mybir.dt.bfloat16
    ALU, ACT, AX = mybir.AluOpType, mybir.ActivationFunctionType, mybir.AxisListType.X

    with ExitStack() as ctx:
        def sb(name, cols, dt=f32, parts=128):
            return ctx.enter_context(nc.sbuf_tensor(name, [parts, cols], dt))

        def sem(name):
            return ctx.enter_context(nc.semaphore(name))

        X0 = sb("X0", BP * REG)
        X2 = sb("X2", BP * REG2)
        Z0 = sb("Z0", BP * REG)
        Z2 = sb("Z2", BP * REG2)
        work = [sb(f"work{i}", WORK) for i in range(5)]
        turned, freqw, specA, specD, backw = work
        tabA = sb("tabA", 1024)
        tabD = sb("tabD", 1024)
        taps = sb("taps", 1024, parts=12)
        parS = sb("parS", P_ALL)
        cstS = sb("cstS", C_ALL)
        wts = sb("wts", 2 * 2 * 3 * C)
        w1S = sb("w1S", 2 * 3 * C)
        w2S = sb("w2S", R * TAPS)
        b1S = sb("b1S", 1)
        selS = sb("selS", TAPS * 128, bf16, parts=3 * R * TAPS)
        idbS = sb("idbS", 128, bf16)
        stats = sb("stats", NCH * 6)
        small = sb("small", 32)
        ksum = sb("ksum", 2 * C)
        lsum = sb("lsum", 128, parts=12)
        psum = ctx.enter_context(nc.psum_tensor("psum", [128, BANKS, N], f32))

        def cm(c, n=128, k=128):
            return cstS[0:k, c:c + n]

        def rows(t, reg, bp, g, n, shift=0, p0=0, p1=128):
            o = bp * reg + g * GROUP + 2 + 2 * shift
            return t[p0:p1, o:o + n * GROUP].rearrange("p (r w) -> p r w", w=GROUP)[:, :, 0:ROW]

        def bank(n):
            return psum[:, n % BANKS, :]

        filled = [sem(f"bank_filled{i}") for i in range(BANKS)]
        drained = [sem(f"bank_drained{i}") for i in range(BANKS)]
        consts_in = sem("consts_in")
        par_in = sem("par_in")
        zeroed = sem("zeroed")
        x_in_sem = [sem(f"x_loaded{i}") for i in range(BP)]
        shifted = [sem(f"shifted{i}") for i in range(BP)]
        x2_in = [sem(f"x2_in{i}") for i in range(BP)]
        z2_in = [sem(f"z2_in{i}") for i in range(BP)]
        relaid = sem("relaid")
        edge_zeros = sem("edge_zeros")
        unlaid = sem("unlaid")
        prep_done = sem("prep_done")
        hid_ready = sem("hid_ready")
        exp_out = sem("exp_out")
        probs_ready = sem("probs_ready")
        pool_sums = sem("pool_sums")
        x_first = sem("x_first")
        edges = sem("edges")
        link_s = sem("dve_link")
        mean_in = sem("mean_in")
        var_in = sem("var_in")
        std_ready = sem("std_ready")
        bn_ready = sem("bn_ready")
        relu_done = sem("relu_done")
        table_done = sem("table_done")
        out_done = sem("out_done")

        hid = work[0]
        lgt, ex = work[1][:, 0:576], work[1][:, 576:1152]
        mx, sm, rc = (work[1][:, 1152 + 64 * i:1216 + 64 * i] for i in range(3))
        pr, rs = work[2][:, 0:576], work[2][:, 576:1152]
        accP = work[2][:, 1152:1152 + N]
        p3 = work[3][:, 0:864].bitcast(bf16)
        pT = work[3][:, 1024:2048].bitcast(bf16)
        pool_slot = [work[4][:, N * i:N * (i + 1)] for i in range(4)]
        pe_slot = [tabA[:, 0:N], tabA[:, N:2 * N], tabD[:, 0:N]]
        two_x_slot = tabD[:, N:2 * N]
        POOL_TAPS = 6
        PE_TAPS = TAPS - POOL_TAPS

        block = ctx.enter_context(nc.Block())

        class Bank:

            def __init__(self, eng, base):
                self.eng, self.base = eng, base

            def claim(self, n):
                if not isinstance(self.base, int) or self.base + n // BANKS > 0:
                    self.eng.wait_ge(drained[n % BANKS], self.base + n // BANKS)

            def full(self, n):
                self.eng.wait_ge(filled[n % BANKS], self.base + n // BANKS + 1)

            def result(self, n):
                self.eng.wait_ge(drained[n % BANKS], self.base + n // BANKS + 1)

        def by_channel(ap):
            return ap.rearrange("p (c h) -> p c h", h=H)

        def by_row(ap):
            return ap.rearrange("p (r w) -> p r w", w=ROW)

        def planar(bp, r=None):
            p0, p1 = (0, 128) if r is None else (C * r, C * r + C)
            return Z2[p0:p1, bp * REG2:bp * REG2 + G * ROW].rearrange("p (g b w) -> p g b w", b=2, w=W)

        def interleaved(t, bp):
            return rows(t, REG, bp, 0, G).rearrange("p g (w b) -> p g b w", b=2)

        def load_x(eng, bp, b2):
            for r in range(R):
                dst = planar(bp, r)[:, :, b2]
                src = x_in[2 * bp + b2].rearrange("c (g r) w -> r c g w", r=R)[r]
                eng.dma_start(dst, src).then_inc(x_in_sem[bp], 16)

        def shift_two(eng, dst, src, bp, done):
            s, d, n = bp * REG, bp * REG2, G * GROUP
            eng.dma_start(dst[0:2 * C, d + GROUP:d + GROUP + n], src[2 * C:128, s:s + n]).then_inc(done, 16)
            eng.dma_start(dst[2 * C:128, d:d + n], src[0:2 * C, s:s + n]).then_inc(done, 16)

        @block.sync
        def _(sp):
            sp.dma_start(cstS[:, :], cst).then_inc(consts_in, 16)
            sp.dma_start(w1S[:, :], w1).then_inc(consts_in, 16)
            for bp in range(BP):
                load_x(sp, bp, 0)
            sp.dma_start(b1S[:, :], b1).then_inc(consts_in, 16)
            sp.dma_start(w2S[:, :], w2).then_inc(consts_in, 16)
            sp.dma_start(selS[:, :], sel).then_inc(consts_in, 16)
            sp.dma_start(idbS[:, :], idb).then_inc(consts_in, 16)
            sp.dma_start(parS[:, :], par[0]).then_inc(par_in, 16)
            sp.wait_ge(zeroed, 1)
            for bp in range(BP):
                sp.wait_ge(relaid, bp + 1)
                shift_two(sp, X2, X0, bp, x2_in[bp])
                s, n = bp * REG, G * GROUP
                m = bp * REG2
                sp.dma_start(Z0[0:3 * C, s:s + n], X0[C:128, s:s + n]).then_inc(shifted[bp], 16)
                sp.dma_start(Z0[3 * C:128, s:s + n - GROUP], X0[0:C, s + GROUP:s + n]).then_inc(shifted[bp], 16)
                sp.wait_ge(edge_zeros, bp + 1)
                sp.dma_start(Z2[C:128, m:m + n], X0[0:3 * C, s:s + n]).then_inc(shifted[bp], 16)
                sp.dma_start(Z2[0:C, m + GROUP:m + n], X0[3 * C:128, s:s + n - GROUP]).then_inc(shifted[bp], 16)
            with sp.Fori(0, DEPTH) as j:
                before = Bank(sp, PRO_ROUNDS + LAY_ROUNDS * (j - 1))
                for bp in range(BP):
                    sp.wait_ge(x_first, Q * bp + Q)
                    for q in range(Q):
                        before.result(LAY["invW", Q * bp + q])
                    shift_two(sp, X2, X0, bp, x2_in[bp])
                sp.wait_ge(prep_done, j + 1)
                sp.dma_start(parS[:, :], par[bass.ds(j + 1, 1)].rearrange("o p c -> (o p) c")).then_inc(par_in, 16)
                for bp in range(BP):
                    sp.wait_ge(relu_done, BP * j + bp + 1)
                    shift_two(sp, Z2, Z0, bp, z2_in[bp])
            for bp in range(BP):
                sp.wait_ge(unlaid, bp + 1)
                for b2 in range(2):
                    for r in range(R):
                        dst = out[2 * bp + b2].rearrange("c (g r) w -> r c g w", r=R)[r]
                        sp.dma_start(dst, planar(bp, r)[:, :, b2]).then_inc(out_done, 16)
            sp.wait_ge(out_done, 16 * B * R)

        @block.gpsimd
        def _(pool):
            def edge(bp):
                pool.wait_ge(relaid, bp + 1)
                nc.gpsimd.memset(Z2[0:2 * C, bp * REG2:bp * REG2 + GROUP], 0.0).then_inc(edge_zeros, 1)

            edge(0)
            edge(1)

            bk = Bank(pool, 0)
            for c in range(NCH):
                bp, q = divmod(c, Q)
                if q == 0 and bp + 2 < BP:
                    edge(bp + 2)
                for k in range(1, POOL_TAPS):
                    if k == 1:
                        bk.result(PRO["spread", bp, q, 0])
                        if c:
                            pool.wait_ge(x_first, c)
                        a = pool_slot[(POOL_TAPS * c) % 4]
                    else:
                        pool.wait_ge(pool_sums, (POOL_TAPS - 1) * c + k - 1)
                        a = accP
                    bk.result(PRO["spread", bp, q, k])
                    nc.gpsimd.tensor_tensor(accP, a, pool_slot[(POOL_TAPS * c + k) % 4], op=ALU.add)\
                        .then_inc(pool_sums, 1)
                pool.wait_ge(pool_sums, (POOL_TAPS - 1) * (c + 1))
                bk.result(PRO["sum", c])
                nc.gpsimd.tensor_tensor(rows(X0, REG, bp, CH * q, CH), by_row(two_x_slot), by_row(accP),
                                        op=ALU.subtract).then_inc(x_first, 1)
            nc.gpsimd.memset(Z2[0:2 * C, :].rearrange("p (b s) -> p b s", s=REG2)[:, :, 0:GROUP], 0.0).then_inc(edges, 1)

        @block.scalar
        def _(act):
            for bp in range(BP):
                load_x(act, bp, 1)
            act.wait_ge(consts_in, 16 * 6)
            bk = Bank(act, 0)

            def hidden(bp):
                for q in range(Q):
                    n = PRO["conv", bp, q]
                    bk.full(n)
                    nc.scalar.activation(hid[:, N * q:N * q + N], bank(n), ACT.Identity,
                                         bias=b1S[:, 0:1]).then_inc(drained[n % BANKS], 1)

            def hidden_then_exp(bp):
                hidden(bp)
                for i in range(2):
                    bk.result(PRO["logits", bp, i])
                nc.scalar.activation(ex, lgt, ACT.Exp).then_inc(exp_out, 1)

            def probs_turn(bp):
                for q in range(Q):
                    n = PRO["probsT", bp, q]
                    bk.full(n)
                    nc.scalar.activation(pT[0:108, N * q:N * q + N], bank(n).bitcast(bf16)[0:108, 0:N],
                                         ACT.Copy).then_inc(drained[n % BANKS], 1)

            def interleave(bp):
                act.wait_ge(x_in_sem[bp], 16 * 2 * R)
                nc.scalar.activation(interleaved(X0, bp), planar(bp), ACT.Identity).then_inc(relaid, 1)

            interleave(0)
            interleave(1)
            hidden_then_exp(0)
            probs_turn(0)
            for bp in range(BP):
                if bp + 2 < BP:
                    interleave(bp + 2)
                if bp + 1 < BP:
                    hidden_then_exp(bp + 1)
                    probs_turn(bp + 1)

            with act.Fori(0, DEPTH) as j:
                bk = Bank(act, PRO_ROUNDS + LAY_ROUNDS * j)
                for c in range(NCH):
                    n = LAY["conv1", c]
                    bk.full(n)
                    nc.scalar.activation(rows(Z0, REG, c // Q, CH * (c % Q), CH), by_row(bank(n)),
                                         ACT.Identity).then_inc(drained[n % BANKS], 1)

                def square(i):
                    n = LAY["table", i]
                    bk.full(n)
                    nc.scalar.activation(turned[:, N * i:N * i + N], bank(n), ACT.Square).then_inc(drained[n % BANKS], 1)

                def root(which):
                    bk.result(LAY["var", which])
                    nc.scalar.activation(small[:, 8:9], small[:, 7:8], ACT.Sqrt).then_inc(std_ready, 1)

                square(0)
                square(1)
                root(1)
                act.wait_ge(bn_ready, 2 * j + 1)
                for bp in range(BP):
                    z = rows(Z0, REG, bp, 0, G)
                    nc.scalar.activation(z, z, ACT.Relu, bias=small[:, 13:14],
                                         scale=small[:, 12:13]).then_inc(relu_done, 1)
                square(2)
                square(3)
                act.wait_ge(table_done, j + 1)
                for k in range(BP + 4):
                    for q in range(Q):
                        if 0 <= k - 4 < BP:
                            c = (k - 4) * Q + q
                            n = LAY["invW", c]
                            if c == 0:
                                act.wait_ge(bn_ready, 2 * j + 2)
                            bk.full(n)
                            nc.scalar.activation(rows(X0, REG, k - 4, CH * q, CH), by_row(bank(n)), ACT.Identity,
                                                 bias=small[:, 13:14], scale=small[:, 12:13]).then_inc(drained[n % BANKS], 1)
                    for q in range(Q):
                        if 0 <= k - 3 < BP:
                            n = LAY["invH", (k - 3) * Q + q]
                            bk.full(n)
                            dst = backw[:, :].rearrange("p (h c) -> p c h", c=C)[:, 8 * q:8 * q + 8, :]
                            nc.scalar.activation(dst, by_channel(bank(n)), ACT.Identity).then_inc(drained[n % BANKS], 1)
                    for q in range(Q):
                        if 0 <= k < BP:
                            n = LAY["turn", k * Q + q]
                            bk.full(n)
                            dst = turned[:, :].rearrange("p (c h) -> p h c", h=H)[:, 16 * q:16 * q + 16, :]
                            nc.scalar.activation(dst, bank(n).rearrange("p (h c) -> p h c", c=C),
                                                 ACT.Identity).then_inc(drained[n % BANKS], 1)
                    if k == 2:
                        root(2)
            bk = Bank(act, PRO_ROUNDS + LAY_ROUNDS * (DEPTH - 1))
            for bp in range(BP):
                for q in range(Q):
                    bk.result(LAY["invW", Q * bp + q])
                nc.scalar.activation(planar(bp), interleaved(X0, bp), ACT.Identity).then_inc(unlaid, 1)

        @block.vector
        def _(dve):
            count = [0, 0]

            def link(ins):
                ins.then_inc(link_s, 1)
                count[0] += 1
                dve.wait_ge(link_s, count[1] + count[0])

            def prepare(layer):
                dve.wait_ge(par_in, 16 * (layer + 1))
                link(nc.vector.tensor_reduce(ksum[:, :], parS[:, P_K:P_F].rearrange("p (k t o) -> p k o t", k=2, t=TAPS),
                                             op=ALU.add, axis=AX))
                for k in range(2):
                    for form in range(2):
                        o = (2 * k + form) * 3 * C
                        w = wts[:, o:o + 3 * C].rearrange("p (d o) -> p d o", o=C)
                        m = ksum[:, C * k:C * k + C].unsqueeze(1).broadcast_to([128, 3, C])
                        f = parS[:, P_F + o:P_F + o + 3 * C].rearrange("p (d o) -> p d o", o=C)
                        nc.vector.scalar_tensor_tensor(w, in0=m, scalar=cstS[:, C_MASK + form:C_MASK + form + 1], in1=f,
                                                       op0=ALU.mult, op1=ALU.add)
                nc.vector.tensor_copy(small[:, 14:16], parS[:, P_GB:P_GB + 2])
                ml = lsum[:, 0:16]
                row = lsum[:, 16:64].rearrange("p (c t) -> p c t", t=3)
                al, be = lsum[:, 64:80], lsum[:, 80:96]
                link(nc.vector.tensor_reduce(ml, parS[0:12, P_L9:P_ALL].rearrange("p (c t) -> p c t", t=TAPS),
                                             op=ALU.add, axis=AX))
                link(nc.vector.scalar_tensor_tensor(row, in0=ml.unsqueeze(2).broadcast_to([12, 16, 3]), scalar=-1.0 / TAPS,
                                                    in1=parS[0:12, P_L:P_L9].rearrange("p (c t) -> p c t", t=3),
                                                    op0=ALU.mult, op1=ALU.add))
                nc.vector.tensor_scalar(al, row[:, :, 1], cstS[0:12, C_ONE:C_ONE + 1], None, ALU.mult)
                link(nc.vector.scalar_tensor_tensor(be, in0=row[:, :, 0], scalar=cstS[0:12, C_SGN:C_SGN + 1],
                                                    in1=row[:, :, 2], op0=ALU.mult, op1=ALU.add))
                t3 = taps[:, :].rearrange("p (c k) -> p c k", k=64)
                link(nc.vector.tensor_tensor(t3, be.unsqueeze(2).broadcast_to([12, 16, 64]),
                                             cstS[0:12, C_CS:C_CS + 64].unsqueeze(1).broadcast_to([12, 16, 64]),
                                             op=ALU.mult))
                nc.vector.tensor_tensor(t3, t3, al.unsqueeze(2).broadcast_to([12, 16, 64]), op=ALU.add)\
                    .then_inc(prep_done, 1)
                dve.wait_ge(prep_done, layer + 1)

            for t in (X0, Z0):
                v = t[:, :].rearrange("p (b s) -> p b s", s=REG)
                nc.vector.memset(v[:, :, 0:G * GROUP].rearrange("p b (r w) -> p b r w", w=GROUP)[:, :, :, 0:2], 0.0)
                nc.vector.memset(v[:, :, G * GROUP:REG], 0.0)
            v = Z0[3 * C:128, :].rearrange("p (b s) -> p b s", s=REG)
            nc.vector.memset(v[:, :, (G - 1) * GROUP + 2:G * GROUP], 0.0)
            v = X2[:, :].rearrange("p (b s) -> p b s", s=REG2)
            nc.vector.memset(v[0:2 * C, :, 0:GROUP], 0.0)
            for t in (X2, Z2):
                v = t[:, :].rearrange("p (b s) -> p b s", s=REG2)
                last = nc.vector.memset(v[:, :, G * GROUP:REG2], 0.0)
            last.then_inc(zeroed, 1)

            dve.wait_ge(consts_in, 16 * 6)
            bk = Bank(dve, 0)
            prepare(0)

            def softmax(bp):
                z3 = lgt.rearrange("p (s k) -> p s k", k=TAPS)
                e3 = ex.rearrange("p (s k) -> p s k", k=TAPS)
                for q in range(Q):
                    bk.result(PRO["conv", bp, q])
                    u = hid[:, N * q:N * q + N]
                    nc.vector.scalar_tensor_tensor(u, in0=u, scalar=LEAK, in1=u, op0=ALU.mult,
                                                   op1=ALU.max).then_inc(hid_ready, 1)
                for i in range(2):
                    n = PRO["logits", bp, i]
                    bk.full(n)
                    link(nc.vector.tensor_reduce(mx[:, 32 * i:32 * i + 32],
                                                 bank(n)[:, 0:288].rearrange("p (s k) -> p s k", k=TAPS), op=ALU.max, axis=AX))
                    ins = nc.vector.tensor_tensor(z3[:, 32 * i:32 * i + 32], bank(n)[:, 0:288].rearrange("p (s k) -> p s k", k=TAPS),
                                                  mx[:, 32 * i:32 * i + 32].unsqueeze(2).broadcast_to([128, 32, TAPS]),
                                                  op=ALU.subtract)
                    ins.then_inc(drained[n % BANKS], 1)
                dve.wait_ge(exp_out, bp + 1)
                link(nc.vector.tensor_reduce(sm, e3, op=ALU.add, axis=AX))
                link(nc.vector.reciprocal(rc, sm))
                link(nc.vector.tensor_tensor(pr.rearrange("p (s k) -> p s k", k=TAPS), e3,
                                             rc.unsqueeze(2).broadcast_to([128, 64, TAPS]), op=ALU.mult))
                part = p3.rearrange("p (g s m) -> p g s m", s=3, m=36)
                p4, r4 = (a.rearrange("p (g m) -> p g m", m=36) for a in (pr, rs))
                if bp:
                    n = PRO["probsT", bp - 1, Q - 1]
                    bk.full(n)
                link(nc.vector.tensor_copy(part[:, :, 0], p4))
                link(nc.vector.tensor_tensor(r4, p4, part[:, :, 0], op=ALU.subtract))
                link(nc.vector.tensor_copy(part[:, :, 1], r4))
                link(nc.vector.tensor_tensor(r4, r4, part[:, :, 1], op=ALU.subtract))
                nc.vector.tensor_copy(part[:, :, 2], r4).then_inc(probs_ready, 1)

            def two_x_less(c):
                n = PRO["sum", c]
                bk.full(n)
                if c:
                    dve.wait_ge(x_first, c)
                nc.vector.scalar_tensor_tensor(by_row(two_x_slot), in0=rows(X0, REG, c // Q, CH * (c % Q), CH), scalar=2.0,
                                               in1=by_row(bank(n)), op0=ALU.mult, op1=ALU.subtract)\
                    .then_inc(drained[n % BANKS], 1)

            softmax(0)
            for bp in range(BP):
                if bp + 1 < BP:
                    softmax(bp + 1)
                dve.wait_ge(shifted[bp], 16 * 4)
                for q in range(Q):
                    c = bp * Q + q
                    for k in range(TAPS):
                        if k == SUM_AT and c:
                            two_x_less(c - 1)
                        di, dj = k // 3, k % 3
                        src = (rows(Z2, REG2, bp, CH * q, CH, dj - 1), rows(X0, REG, bp, CH * q, CH, dj - 1),
                               rows(Z0, REG, bp, CH * q, CH, dj - 1))[di]
                        n = PRO["spread", bp, q, k]
                        bk.full(n)
                        if k < POOL_TAPS:
                            m = POOL_TAPS * c + k
                            if m >= 4:
                                dve.wait_ge(pool_sums, (POOL_TAPS - 1) * ((m - 4) // POOL_TAPS) + max((m - 4) % POOL_TAPS, 1))
                            dst = pool_slot[m % 4]
                        else:
                            dst = pe_slot[k - POOL_TAPS]
                        nc.vector.tensor_tensor(by_row(dst), src, by_row(bank(n)), op=ALU.mult)\
                            .then_inc(drained[n % BANKS], 1)
            two_x_less(NCH - 1)

            with dve.Fori(0, DEPTH) as j:
                assert count[0] == PRO_LINKS, count
                count[0], count[1] = 0, PRO_LINKS + LAY_LINKS * j
                bk = Bank(dve, PRO_ROUNDS + LAY_ROUNDS * j)
                S = lambda i: small[:, i:i + 1]

                def aggregate():
                    nc.vector.tensor_copy(S(16), S(14))
                    nc.vector.bn_aggr(small[:, 0:2], stats[:, :]).then_inc(mean_in, 1)

                def spread_of_means(which):
                    n = LAY["mean", which]
                    bk.full(n)
                    nc.vector.tensor_copy(S(2), bank(n)[:, 0:1]).then_inc(drained[n % BANKS], 1)
                    bk.result(n)
                    link(nc.vector.tensor_tensor(S(3), S(0), S(2), op=ALU.subtract))
                    nc.vector.scalar_tensor_tensor(S(4), in0=S(3), scalar=S(3), in1=S(1), op0=ALU.mult,
                                                   op1=ALU.add).then_inc(var_in, 1)

                def variance(which):
                    n = LAY["var", which]
                    bk.full(n)
                    nc.vector.tensor_scalar(S(7), bank(n)[:, 0:1], BN_EPS, None, ALU.add).then_inc(drained[n % BANKS], 1)

                def scale_and_bias(which):
                    dve.wait_ge(std_ready, 2 * j + which)
                    link(nc.vector.reciprocal(S(9), S(8)))
                    link(nc.vector.tensor_tensor(S(10), S(9), S(9), op=ALU.mult))
                    link(nc.vector.tensor_tensor(S(10), S(10), S(7), op=ALU.mult))
                    link(nc.vector.tensor_scalar(S(10), S(10), -0.5, 1.5, ALU.mult, ALU.add))
                    link(nc.vector.tensor_tensor(S(9), S(9), S(10), op=ALU.mult))
                    link(nc.vector.tensor_tensor(S(12), S(9), S(14), op=ALU.mult))
                    link(nc.vector.tensor_tensor(S(11), S(2), S(12), op=ALU.mult))
                    nc.vector.tensor_tensor(S(13), S(15), S(11), op=ALU.subtract).then_inc(bn_ready, 1)

                for c in range(NCH):
                    bk.result(LAY["conv1", c])
                    ins = nc.vector.bn_stats(stats[:, 6 * c:6 * c + 6], rows(Z0, REG, c // Q, CH * (c % Q), CH))
                link(ins)
                aggregate()
                spread_of_means(1)
                variance(1)
                scale_and_bias(1)

                for i in range(4):
                    bk.result(LAY["table", i])
                half = freqw[:, 0:1024]
                link(nc.vector.tensor_tensor(half, turned[:, 0:1024], turned[:, 1024:2048], op=ALU.add))
                link(nc.vector.tensor_scalar(half, half, 2 * STEP, 2.0, ALU.mult, ALU.add))
                link(nc.vector.reciprocal(half, half))
                h3 = half.rearrange("p (c k) -> p c k", k=64)
                a3, d3 = (t[:, :].rearrange("p (c k) -> p c k", k=64) for t in (tabA, tabD))
                nc.vector.tensor_tensor(a3, h3, h3[:, :, ::-1], op=ALU.add)
                link(nc.vector.tensor_tensor(d3, h3[:, :, ::-1], h3, op=ALU.subtract))
                nc.vector.tensor_scalar(a3[:, :, 0:64:63], h3[:, :, 0:64:63], 2.0, None, ALU.mult)
                nc.vector.tensor_scalar(d3[:, :, 0:64:63], d3[:, :, 0:64:63], 0.0, None, ALU.mult).then_inc(table_done, 1)
                dve.wait_ge(table_done, j + 1)

                for c in range(NCH):
                    n = LAY["conv2", c]
                    bk.full(n)
                    xc = rows(X0, REG, c // Q, CH * (c % Q), CH)
                    nc.vector.scalar_tensor_tensor(xc, in0=by_row(bank(n)), scalar=STEP, in1=xc, op0=ALU.mult,
                                                   op1=ALU.add).then_inc(drained[n % BANKS], 1)
                    bk.result(n)
                    ins = nc.vector.bn_stats(stats[:, 6 * c:6 * c + 6], xc)
                link(ins)
                aggregate()
                for k in range(BP + 4):
                    for q in range(Q):
                        if 0 <= k - 2 < BP:
                            n = LAY["fwdH", (k - 2) * Q + q]
                            bk.full(n)
                            src = bank(n).rearrange("p (c b k) -> p c b k", c=4, b=2)
                            for t, dst in ((tabA, specA), (tabD, specD)):
                                tt = t[:, 256 * q:256 * q + 256].rearrange("p (c k) -> p c k", k=64)\
                                    .unsqueeze(2).broadcast_to([128, 4, 2, 64])
                                to = dst[:, N * q:N * q + N].rearrange("p (c b k) -> p c b k", c=4, b=2)
                                if dst is specD:
                                    to = to[:, :, :, ::-1]
                                ins = nc.vector.tensor_tensor(to, src, tt, op=ALU.mult)
                            ins.then_inc(drained[n % BANKS], 1)
                    for q in range(Q):
                        if 0 <= k - 1 < BP:
                            n = LAY["fwdW", (k - 1) * Q + q]
                            bk.full(n)
                            nc.vector.tensor_copy(freqw[:, N * q:N * q + N], bank(n)).then_inc(drained[n % BANKS], 1)
                    if k == 1:
                        spread_of_means(2)
                    if k == 2:
                        variance(2)
                    if k == 3:
                        scale_and_bias(2)
                        prepare(j + 1)
                assert count[0] == LAY_LINKS, count

        @block.tensor
        def _(pe):
            def conv(bk, n, c, X, X2_, weights, form_stride):
                bp, q = divmod(c, Q)
                bk.claim(n)
                out_b = bank(n)
                for dj in range(3):
                    for r in range(R):
                        form, src, g = ((1, X2_, CH * q), (0, X, CH * q), (1, X, CH * q), (0, X2_, CH * q + 1))[r]
                        reg = REG2 if r in (0, 3) else REG
                        o = form * form_stride + dj * C
                        last = nc.tensor.matmul(out_b[C * r:C * r + C, :], weights[:, o:o + C],
                                                rows(src, reg, bp, g, CH, dj - 1), start=(dj == 0), stop=(dj == 2),
                                                tile_position=(0, C * r))
                last.then_inc(filled[n % BANKS], 1)

            bk = Bank(pe, 0)
            pe.wait_ge(consts_in, 16 * 6)
            pe.wait_ge(zeroed, 1)

            def predictor(bp):
                pe.wait_ge(x2_in[bp], 32)
                for q in range(Q):
                    conv(bk, PRO["conv", bp, q], bp * Q + q, X0, X2, w1S, 3 * C)
                for i in range(2):
                    n = PRO["logits", bp, i]
                    bk.claim(n)
                    pe.wait_ge(hid_ready, Q * bp + 2 * i + 2)
                    for g in range(8):
                        p = (8 * i + g) * 128
                        last = nc.tensor.matmul(bank(n)[:, 36 * g:36 * g + 36], hid[:, p:p + 128], w2S[:, :],
                                                start=True, stop=True)
                    last.then_inc(filled[n % BANKS], 1)

            def turn_probs(bp):
                pe.wait_ge(probs_ready, bp + 1)
                for q in range(Q):
                    n = PRO["probsT", bp, q]
                    bk.claim(n)
                    for g in range(CH):
                        p = (CH * q + g) * 108
                        last = nc.tensor.transpose(bank(n).bitcast(bf16)[0:108, 128 * g:128 * g + 128], p3[:, p:p + 108],
                                                   idbS[:, :])
                    last.then_inc(filled[n % BANKS], 1)

            def add_up(c):
                n = PRO["sum", c]
                bk.claim(n)
                for k in range(POOL_TAPS, TAPS):
                    bk.result(PRO["spread", c // Q, c % Q, k])
                for i in range(PE_TAPS):
                    last = nc.tensor.matmul(bank(n), cm(C_ID), pe_slot[i], start=(i == 0), stop=(i == PE_TAPS - 1))
                last.then_inc(filled[n % BANKS], 1)

            predictor(0)
            turn_probs(0)
            for bp in range(BP):
                if bp + 1 < BP:
                    predictor(bp + 1)
                for q in range(Q):
                    bk.result(PRO["probsT", bp, q])
                    for k in range(TAPS):
                        if k == SUM_AT and bp * Q + q > 0:
                            add_up(bp * Q + q - 1)
                        n = PRO["spread", bp, q, k]
                        bk.claim(n)
                        nc.tensor.matmul(bank(n), selS[:, 128 * k:128 * k + 128], pT[0:108, N * q:N * q + N],
                                         start=True, stop=True).then_inc(filled[n % BANKS], 1)
                if bp + 1 < BP:
                    turn_probs(bp + 1)
            add_up(NCH - 1)

            with pe.Fori(0, DEPTH) as j:
                bk = Bank(pe, PRO_ROUNDS + LAY_ROUNDS * j)
                pe.wait_ge(prep_done, j + 1)
                for c in range(NCH):
                    if c % Q == 0:
                        pe.wait_ge(x2_in[c // Q], 32 * (j + 2))
                    conv(bk, LAY["conv1", c], c, X0, X2, wts, 3 * C)

                def table(i):
                    n = LAY["table", i]
                    bk.claim(n)
                    e = (C_ERE, C_EIM)[i // 2]
                    nc.tensor.matmul(bank(n), cm(e, k=12), taps[:, N * (i % 2):N * (i % 2) + N], start=True,
                                     stop=True).then_inc(filled[n % BANKS], 1)

                def average(what, which, sem_, col):
                    n = LAY[what, which]
                    bk.claim(n)
                    pe.wait_ge(sem_, 2 * j + which)
                    nc.tensor.matmul(bank(n)[:, 0:1], cm(C_AVG), small[:, col:col + 1], start=True,
                                     stop=True).then_inc(filled[n % BANKS], 1)

                table(0)
                average("mean", 1, mean_in, 0)
                table(1)
                average("var", 1, var_in, 4)
                table(2)
                table(3)
                pe.wait_ge(edges, 1)
                for c in range(NCH):
                    if c % Q == 0:
                        pe.wait_ge(relu_done, BP * j + c // Q + 1)
                        pe.wait_ge(z2_in[c // Q], 32 * (j + 1))
                    conv(bk, LAY["conv2", c], c, Z0, Z2, wts[:, 2 * 3 * C:], 3 * C)
                for k in range(BP + 4):
                    for q in range(Q):
                        if 0 <= k - 4 < BP:
                            c = (k - 4) * Q + q
                            n = LAY["invW", c]
                            bk.claim(n)
                            for i in range(Q):
                                bk.result(LAY["invH", (k - 4) * Q + i])
                            for g in range(CH):
                                p = (CH * q + g) * 128
                                last = nc.tensor.matmul(bank(n)[:, 128 * g:128 * g + 128], backw[:, p:p + 128], cm(C_IW),
                                                        start=True, stop=True)
                            last.then_inc(filled[n % BANKS], 1)
                    for q in range(Q):
                        if 0 <= k - 3 < BP:
                            c = (k - 3) * Q + q
                            n = LAY["invH", c]
                            bk.claim(n)
                            bk.result(LAY["fwdH", c])
                            for cp in range(4):
                                p = N * q + 128 * cp
                                o = bank(n)[:, 128 * cp:128 * cp + 128]
                                nc.tensor.matmul(o, specA[:, p:p + 128], cm(C_FH), start=True, stop=False)
                                last = nc.tensor.matmul(o, specD[:, p:p + 128], cm(C_IR), start=False, stop=True)
                            last.then_inc(filled[n % BANKS], 1)
                    for q in range(Q):
                        if 0 <= k - 2 < BP:
                            c = (k - 2) * Q + q
                            n = LAY["fwdH", c]
                            bk.claim(n)
                            bk.result(LAY["fwdW", c])
                            nc.tensor.matmul(bank(n), cm(C_FH), freqw[:, N * q:N * q + N], start=True,
                                             stop=True).then_inc(filled[n % BANKS], 1)
                    for q in range(Q):
                        if 0 <= k - 1 < BP:
                            c = (k - 1) * Q + q
                            n = LAY["fwdW", c]
                            bk.claim(n)
                            for i in range(Q):
                                bk.result(LAY["turn", (k - 1) * Q + i])
                            for i in range(4):
                                p = (4 * q + i) * 128
                                last = nc.tensor.matmul(bank(n)[:, 128 * i:128 * i + 128], turned[:, p:p + 128],
                                                        cm(C_FW), start=True, stop=True)
                            last.then_inc(filled[n % BANKS], 1)
                    for q in range(Q):
                        if 0 <= k < BP:
                            c = k * Q + q
                            n = LAY["turn", c]
                            bk.claim(n)
                            bk.result(LAY["conv2", c])
                            for g in range(CH):
                                last = nc.tensor.transpose(bank(n)[:, 128 * g:128 * g + 128],
                                                           rows(X0, REG, k, CH * q + g, 1)[:, 0], cm(C_ID))
                            last.then_inc(filled[n % BANKS], 1)
                    if k == 1:
                        average("mean", 2, mean_in, 0)
                    if k == 2:
                        average("var", 2, var_in, 4)


def constants():
    n = np.arange(64)
    th = 2 * np.pi / 64
    freq = np.array([p if p <= 31 else (p - 63 if p < 63 else 32) for p in range(64)])

    def cas(a):
        return (np.cos(a) + np.sin(a)) / 8

    c = np.zeros((128, C_ALL), np.float64)
    two = np.eye(2)
    c[:, C_ID:C_ID + 128] = np.eye(128)
    fw = cas(th * np.outer(n, freq))
    c[:, C_FW:C_FW + 128] = np.kron(two, fw).reshape(2, 64, 128).transpose(1, 0, 2).reshape(128, 128)
    c[:, C_FH:C_FH + 128] = np.kron(two, cas(th * np.outer(n, n)))
    c[:, C_IR:C_IR + 128] = np.kron(two, cas(-th * np.outer(n, n)))
    c[:, C_IW:C_IW + 128] = c[:, C_FW:C_FW + 128].T
    c[:, C_AVG:C_AVG + 128] = np.kron(np.ones((R, R)), np.eye(C)) / R
    for c2 in range(2):
        for i in range(3):
            q = c2 * 6 + i * 2
            a = th * n * (i - 1)
            s = slice(64 * c2, 64 * c2 + 64)
            c[q, C_ERE:C_ERE + 128][s], c[q + 1, C_ERE:C_ERE + 128][s] = np.cos(a), -np.sin(a)
            c[q, C_EIM:C_EIM + 128][s], c[q + 1, C_EIM:C_EIM + 128][s] = np.sin(a), np.cos(a)
            c[q, C_CS:C_CS + 64], c[q + 1, C_CS:C_CS + 64] = np.cos(th * freq), np.sin(th * freq)
            c[q, C_ONE] = 1
            c[q, C_SGN], c[q + 1, C_SGN] = 1, -1
    for form in range(2):
        c[C * form:C * (form + 3), C_MASK + form] = -1.0 / TAPS
    sel = np.zeros((3, R, TAPS, TAPS, R, C), np.float32)
    for r in range(R):
        for k in range(TAPS):
            sel[:, r, k, k, r, :] = 1
    return c.astype(np.float32), sel.reshape(3 * R * TAPS, TAPS * 128), np.eye(128, dtype=np.float32)


def windows(k):
    o = np.zeros((R, k.shape[1], 2, 3, k.shape[3]), np.float32)
    for form in range(2):
        for di in range(3):
            o[di + form, :, form] = k[di]
    return o.reshape(128, -1)


def kernel(x, L0_conv_w1, L0_conv_b1, L0_conv_w2, L0_conv_b2, L1_conv_K, L1_conv_L, L1_conv_gamma, L1_conv_beta):
    import ml_dtypes
    import concourse.bacc as bacc
    from concourse.bass_utils import run_bass_kernel_spmd

    x, w1, b1, w2, b2, K, L, gamma, beta = (np.asarray(a) for a in (
        x, L0_conv_w1, L0_conv_b1, L0_conv_w2, L0_conv_b2, L1_conv_K, L1_conv_L, L1_conv_gamma, L1_conv_beta))
    cst, sel, idb = constants()
    par = np.zeros((DEPTH + 1, 128, P_ALL), np.float32)
    for j in range(DEPTH):
        for k, kern in enumerate((K[j].transpose(2, 1, 3, 0), K[j].transpose(2, 0, 3, 1)[::-1, :, ::-1])):
            flat = kern.transpose(1, 0, 2, 3).reshape(C, -1)
            for r in range(R):
                par[j, C * r:C * r + C, P_K + k * TAPS * C:P_K + (k + 1) * TAPS * C] = flat
            par[j, :, P_F + k * 6 * C:P_F + (k + 1) * 6 * C] = windows(kern)
        for r in range(R):
            par[j, C * r:C * r + C, P_GB] = gamma[j]
            par[j, C * r:C * r + C, P_GB + 1] = beta[j]
        for c2 in range(2):
            for i in range(3):
                for tr in range(2):
                    q = c2 * 6 + i * 2 + tr
                    par[j, q, P_L:P_L9] = L[j, c2::2, 0, i, :].reshape(-1)
                    par[j, q, P_L9:P_ALL] = L[j, c2::2, 0].reshape(-1)
    w1p = np.zeros((3, C, 3, C), np.float32)
    w1p[:, :, :, 0:HID] = w1.transpose(2, 1, 3, 0)
    b1p = np.zeros((R, C, 1), np.float32)
    b1p[:, 0:HID, 0] = b1
    b1p[:, HID, 0] = 1.0
    w2p = np.zeros((R, C, R, TAPS), np.float32)
    for r in range(R):
        w2p[r, 0:HID, r] = w2[:, :, 0, 0].T
        w2p[r, HID, r] = b2
    arrays = {
        "x": x, "par": par, "w1": windows(w1p), "b1": b1p.reshape(128, 1), "w2": w2p.reshape(128, R * TAPS),
        "cst": cst, "sel": sel.astype(ml_dtypes.bfloat16), "idb": idb.astype(ml_dtypes.bfloat16),
    }
    nc = bacc.Bacc("TRN2", target_bir_lowering=False, num_devices=1)
    args = [nc.dram_tensor(n, a.shape, mybir.dt.from_np(a.dtype), kind="ExternalInput").ap() for n, a in arrays.items()]
    out = nc.dram_tensor("out", (B, C, H, W), mybir.dt.float32, kind="ExternalOutput").ap()
    build(nc, *args, out)
    r = run_bass_kernel_spmd(nc, [arrays], core_ids=[0])
    return r.results[0]["out"]
```

```python
import numpy as np
import concourse.bass as bass
from concourse import mybir
from contextlib import ExitStack

B, C, H, W = 8, 32, 64, 64
R = 128 // C
G = H // R
BP = B // 2
TAPS = 9
SUM_AT = 5
HID = C // 2
DEPTH = 4
STEP = 0.1
BN_EPS = 1e-5
LEAK = 0.2

ROW = 2 * W
GROUP = ROW + 2
REG = G * GROUP + 4
REG2 = (G + 1) * GROUP + 4
CH = 4
Q = G // CH
NCH = BP * Q
N = CH * ROW
BANKS = 8
WORK = 2048

C_ID, C_FW, C_FH, C_IR, C_IW, C_AVG, C_ERE, C_EIM = (128 * i for i in range(8))
C_CS = 8 * 128
C_ONE = C_CS + 64
C_SGN = C_ONE + 1
C_MASK = C_SGN + 1
C_ALL = C_MASK + 2
P_K = 0
P_F = P_K + 2 * TAPS * C
P_GB = P_F + 2 * 2 * 3 * C
P_L = P_GB + 2
P_L9 = P_L + (C // 2) * 3
P_ALL = P_L9 + (C // 2) * TAPS


def prologue_schedule():
    order = []
    for q in range(Q):
        order.append(("conv", 0, q))
        if q % 2:
            order.append(("logits", 0, q // 2))
    order += [("probsT", 0, 0), ("probsT", 0, 1)]
    for bp in range(BP):
        for q in range(Q):
            order += [("spread", bp, q, k) for k in range(SUM_AT)]
            if bp * Q + q > 0:
                order.append(("sum", bp * Q + q - 1))
            if q == 2 and bp + 1 < BP:
                order.append(("logits", bp + 1, 0))
            if q == 0 and bp > 0:
                order.append(("logits", bp, 1))
            order += [("spread", bp, q, k) for k in range(SUM_AT, TAPS)]
            if q == 1:
                order += [("probsT", bp, 2), ("probsT", bp, 3)]
            if bp + 1 < BP:
                if q == 3:
                    order += [("probsT", bp + 1, 0), ("probsT", bp + 1, 1)]
                order.append(("conv", bp + 1, q))
    order.append(("sum", NCH - 1))
    return order


def layer_schedule():
    order = [("conv1", c) for c in range(NCH)]
    order += [("table", 0), ("mean", 1), ("table", 1), ("var", 1), ("table", 2), ("table", 3)]
    order += [("conv2", c) for c in range(NCH)]
    for k in range(BP + 4):
        for stage, lag in (("invW", 4), ("invH", 3), ("fwdH", 2), ("fwdW", 1), ("turn", 0)):
            if 0 <= k - lag < BP:
                order += [(stage, (k - lag) * Q + q) for q in range(Q)]
        if k == 1:
            order.append(("mean", 2))
        if k == 2:
            order.append(("var", 2))
    return order


PRO = {step: n for n, step in enumerate(prologue_schedule())}
LAY = {step: n for n, step in enumerate(layer_schedule())}
PRO_ROUNDS = len(PRO) // BANKS
LAY_ROUNDS = len(LAY) // BANKS
assert PRO_ROUNDS * BANKS == len(PRO) and LAY_ROUNDS * BANKS == len(LAY)
PRO_LINKS, LAY_LINKS = 69, 27


def build(nc, x_in, par, w1, b1, w2, cst, sel, idb, out):
    f32, bf16 = mybir.dt.float32, mybir.dt.bfloat16
    ALU, ACT, AX = mybir.AluOpType, mybir.ActivationFunctionType, mybir.AxisListType.X

    with ExitStack() as ctx:
        def sb(name, cols, dt=f32, parts=128):
            return ctx.enter_context(nc.sbuf_tensor(name, [parts, cols], dt))

        def sem(name):
            return ctx.enter_context(nc.semaphore(name))

        X0 = sb("X0", BP * REG)
        X2 = sb("X2", BP * REG2)
        Z0 = sb("Z0", BP * REG)
        Z2 = sb("Z2", BP * REG2)
        work = [sb(f"work{i}", WORK) for i in range(5)]
        turned, freqw, specA, specD, backw = work
        tabA = sb("tabA", 1024)
        tabD = sb("tabD", 1024)
        spare = sb("spare", 3 * N)
        taps = sb("taps", 1024, parts=12)
        parS = sb("parS", P_ALL)
        cstS = sb("cstS", C_ALL)
        wts = sb("wts", 2 * 2 * 3 * C)
        w1S = sb("w1S", 2 * 3 * C)
        w2S = sb("w2S", R * TAPS)
        b1S = sb("b1S", 1)
        selS = sb("selS", TAPS * 128, bf16, parts=3 * R * TAPS)
        idbS = sb("idbS", 128, bf16)
        stats = sb("stats", NCH * 6)
        small = sb("small", 32)
        ksum = sb("ksum", 2 * C)
        lsum = sb("lsum", 128, parts=12)
        psum = ctx.enter_context(nc.psum_tensor("psum", [128, BANKS, N], f32))

        def cm(c, n=128, k=128):
            return cstS[0:k, c:c + n]

        def rows(t, reg, bp, g, n, shift=0, p0=0, p1=128):
            o = bp * reg + g * GROUP + 2 + 2 * shift
            return t[p0:p1, o:o + n * GROUP].rearrange("p (r w) -> p r w", w=GROUP)[:, :, 0:ROW]

        def bank(n):
            return psum[:, n % BANKS, :]

        filled = [sem(f"bank_filled{i}") for i in range(BANKS)]
        drained = [sem(f"bank_drained{i}") for i in range(BANKS)]
        consts_in = sem("consts_in")
        par_in = sem("par_in")
        zeroed = sem("zeroed")
        x_in_sem = [sem(f"x_loaded{i}") for i in range(BP)]
        shifted = [sem(f"shifted{i}") for i in range(BP)]
        x2_in = [sem(f"x2_in{i}") for i in range(BP)]
        z2_in = [sem(f"z2_in{i}") for i in range(BP)]
        relaid = sem("relaid")
        edge_zeros = sem("edge_zeros")
        unlaid = sem("unlaid")
        prep_done = sem("prep_done")
        hid_ready = sem("hid_ready")
        exp_out = sem("exp_out")
        probs_ready = sem("probs_ready")
        pool_sums = sem("pool_sums")
        x_first = sem("x_first")
        edges = sem("edges")
        link_s = sem("dve_link")
        mean_in = sem("mean_in")
        var_in = sem("var_in")
        std_ready = sem("std_ready")
        bn_ready = sem("bn_ready")
        relu_done = sem("relu_done")
        table_done = sem("table_done")
        out_done = sem("out_done")

        hid = work[0]
        lgt, ex = work[1][:, 0:576], work[1][:, 576:1152]
        mx, sm, rc = (work[1][:, 1152 + 64 * i:1216 + 64 * i] for i in range(3))
        pr, rs = work[2][:, 0:576], work[2][:, 576:1152]
        accP = [work[2][:, 1152:1152 + N], work[1][:, 1344:1344 + N]]
        p3 = work[3][:, 0:864].bitcast(bf16)
        pT = work[3][:, 1024:2048].bitcast(bf16)
        pool_slot = [work[4][:, N * i:N * (i + 1)] for i in range(4)]
        pe_slot = [tabA[:, 0:N], tabA[:, N:2 * N], tabD[:, 0:N]] + [spare[:, N * i:N * i + N] for i in range(3)]
        two_x_slot = tabD[:, N:2 * N]
        PE_TAPS = (2, 5, 8)
        POOL_TAPS = [k for k in range(TAPS) if k not in PE_TAPS]
        NP = len(POOL_TAPS)

        block = ctx.enter_context(nc.Block())

        class Bank:

            def __init__(self, eng, base):
                self.eng, self.base = eng, base

            def claim(self, n):
                if not isinstance(self.base, int) or self.base + n // BANKS > 0:
                    self.eng.wait_ge(drained[n % BANKS], self.base + n // BANKS)

            def full(self, n):
                self.eng.wait_ge(filled[n % BANKS], self.base + n // BANKS + 1)

            def result(self, n):
                self.eng.wait_ge(drained[n % BANKS], self.base + n // BANKS + 1)

        def by_channel(ap):
            return ap.rearrange("p (c h) -> p c h", h=H)

        def by_row(ap):
            return ap.rearrange("p (r w) -> p r w", w=ROW)

        def planar(bp, r=None):
            p0, p1 = (0, 128) if r is None else (C * r, C * r + C)
            return Z2[p0:p1, bp * REG2:bp * REG2 + G * ROW].rearrange("p (g b w) -> p g b w", b=2, w=W)

        def interleaved(t, bp):
            return rows(t, REG, bp, 0, G).rearrange("p g (w b) -> p g b w", b=2)

        def load_x(eng, bp, b2):
            for r in range(R):
                dst = planar(bp, r)[:, :, b2]
                src = x_in[2 * bp + b2].rearrange("c (g r) w -> r c g w", r=R)[r]
                eng.dma_start(dst, src).then_inc(x_in_sem[bp], 16)

        def shift_two(eng, dst, src, bp, done):
            s, d, n = bp * REG, bp * REG2, G * GROUP
            eng.dma_start(dst[0:2 * C, d + GROUP:d + GROUP + n], src[2 * C:128, s:s + n]).then_inc(done, 16)
            eng.dma_start(dst[2 * C:128, d:d + n], src[0:2 * C, s:s + n]).then_inc(done, 16)

        @block.sync
        def _(sp):
            load_x(sp, 0, 0)
            sp.dma_start(w1S[:, :], w1).then_inc(consts_in, 16)
            sp.dma_start(b1S[:, :], b1).then_inc(consts_in, 16)
            sp.dma_start(w2S[:, :], w2).then_inc(consts_in, 16)
            sp.dma_start(selS[:, :], sel).then_inc(consts_in, 16)
            sp.dma_start(idbS[:, :], idb).then_inc(consts_in, 16)
            sp.dma_start(cstS[:, :], cst).then_inc(consts_in, 16)
            sp.wait_ge(zeroed, 1)
            for bp in range(BP):
                sp.wait_ge(relaid, bp + 1)
                shift_two(sp, X2, X0, bp, x2_in[bp])
                s, n = bp * REG, G * GROUP
                m = bp * REG2
                sp.dma_start(Z0[0:3 * C, s:s + n], X0[C:128, s:s + n]).then_inc(shifted[bp], 16)
                sp.dma_start(Z0[3 * C:128, s:s + n - GROUP], X0[0:C, s + GROUP:s + n]).then_inc(shifted[bp], 16)
                sp.wait_ge(edge_zeros, bp + 1)
                sp.dma_start(Z2[C:128, m:m + n], X0[0:3 * C, s:s + n]).then_inc(shifted[bp], 16)
                sp.dma_start(Z2[0:C, m + GROUP:m + n], X0[3 * C:128, s:s + n - GROUP]).then_inc(shifted[bp], 16)
                if bp + 1 < BP:
                    load_x(sp, bp + 1, 0)
                    load_x(sp, bp + 1, 1)
                if bp == 0:
                    sp.dma_start(parS[:, :], par[0]).then_inc(par_in, 16)
            with sp.Fori(0, DEPTH) as j:
                before = Bank(sp, PRO_ROUNDS + LAY_ROUNDS * (j - 1))
                for bp in range(BP):
                    sp.wait_ge(x_first, Q * bp + Q)
                    for q in range(Q):
                        before.result(LAY["invW", Q * bp + q])
                    shift_two(sp, X2, X0, bp, x2_in[bp])
                sp.wait_ge(prep_done, j + 1)
                sp.dma_start(parS[:, :], par[bass.ds(j + 1, 1)].rearrange("o p c -> (o p) c")).then_inc(par_in, 16)
                for bp in range(BP):
                    sp.wait_ge(relu_done, BP * j + bp + 1)
                    shift_two(sp, Z2, Z0, bp, z2_in[bp])
            for bp in range(BP):
                sp.wait_ge(unlaid, bp + 1)
                for b2 in range(2):
                    for r in range(R):
                        dst = out[2 * bp + b2].rearrange("c (g r) w -> r c g w", r=R)[r]
                        sp.dma_start(dst, planar(bp, r)[:, :, b2]).then_inc(out_done, 16)
            sp.wait_ge(out_done, 16 * B * R)

        @block.gpsimd
        def _(pool):
            def edge(bp):
                pool.wait_ge(relaid, bp + 1)
                nc.gpsimd.memset(Z2[0:2 * C, bp * REG2:bp * REG2 + GROUP], 0.0).then_inc(edge_zeros, 1)

            edge(0)
            edge(1)

            bk = Bank(pool, 0)

            def finish(c):
                if c < 0:
                    return
                pool.wait_ge(pool_sums, (NP - 1) * (c + 1))
                bk.result(PRO["sum", c])
                nc.gpsimd.tensor_tensor(rows(X0, REG, c // Q, CH * (c % Q), CH), by_row(two_x_slot), by_row(accP[c % 2]),
                                        op=ALU.subtract).then_inc(x_first, 1)

            for c in range(NCH):
                bp, q = divmod(c, Q)
                if q == 1 and bp + 2 < BP:
                    edge(bp + 2)
                for k in range(1, NP):
                    if k == 1:
                        bk.result(PRO["spread", bp, q, 0])
                        if c >= 2:
                            pool.wait_ge(x_first, c - 1)
                        a = pool_slot[(NP * c) % 4]
                    else:
                        pool.wait_ge(pool_sums, (NP - 1) * c + k - 1)
                        a = accP[c % 2]
                    bk.result(PRO["spread", bp, q, POOL_TAPS[k]])
                    nc.gpsimd.tensor_tensor(accP[c % 2], a, pool_slot[(NP * c + k) % 4], op=ALU.add)\
                        .then_inc(pool_sums, 1)
                    if k == 3:
                        finish(c - 1)
            finish(NCH - 1)
            nc.gpsimd.memset(Z2[0:2 * C, :].rearrange("p (b s) -> p b s", s=REG2)[:, :, 0:GROUP], 0.0).then_inc(edges, 1)

        @block.scalar
        def _(act):
            load_x(act, 0, 1)
            act.wait_ge(consts_in, 16 * 6)
            bk = Bank(act, 0)

            def hidden(bp, q):
                n = PRO["conv", bp, q]
                bk.full(n)
                nc.scalar.activation(hid[:, N * q:N * q + N], bank(n), ACT.Identity,
                                     bias=b1S[:, 0:1]).then_inc(drained[n % BANKS], 1)

            def exps(bp, i):
                bk.result(PRO["logits", bp, i])
                nc.scalar.activation(ex[:, 288 * i:288 * i + 288], lgt[:, 288 * i:288 * i + 288],
                                     ACT.Exp).then_inc(exp_out, 1)

            def probs_turn(bp, q):
                n = PRO["probsT", bp, q]
                bk.full(n)
                nc.scalar.activation(pT[0:108, N * q:N * q + N], bank(n).bitcast(bf16)[0:108, 0:N],
                                     ACT.Copy).then_inc(drained[n % BANKS], 1)

            def interleave(bp):
                act.wait_ge(x_in_sem[bp], 16 * 2 * R)
                nc.scalar.activation(interleaved(X0, bp), planar(bp), ACT.Identity).then_inc(relaid, 1)

            interleave(0)
            for q in range(Q):
                hidden(0, q)
                if q % 2:
                    exps(0, q // 2)
            interleave(1)
            probs_turn(0, 0)
            probs_turn(0, 1)
            for bp in range(BP):
                for q in range(Q):
                    if q == 1:
                        probs_turn(bp, 2)
                        probs_turn(bp, 3)
                    if bp + 1 < BP:
                        if q == 3:
                            probs_turn(bp + 1, 0)
                            probs_turn(bp + 1, 1)
                        hidden(bp + 1, q)
                        if q == 2:
                            exps(bp + 1, 0)
                    if q == 0 and bp > 0:
                        exps(bp, 1)
                    if q == 0 and bp + 2 < BP:
                        interleave(bp + 2)

            with act.Fori(0, DEPTH) as j:
                bk = Bank(act, PRO_ROUNDS + LAY_ROUNDS * j)
                for c in range(NCH):
                    n = LAY["conv1", c]
                    bk.full(n)
                    nc.scalar.activation(rows(Z0, REG, c // Q, CH * (c % Q), CH), by_row(bank(n)),
                                         ACT.Identity).then_inc(drained[n % BANKS], 1)

                def square(i):
                    n = LAY["table", i]
                    bk.full(n)
                    nc.scalar.activation(turned[:, N * i:N * i + N], bank(n), ACT.Square).then_inc(drained[n % BANKS], 1)

                def root(which):
                    bk.result(LAY["var", which])
                    nc.scalar.activation(small[:, 8:9], small[:, 7:8], ACT.Sqrt).then_inc(std_ready, 1)

                square(0)
                square(1)
                root(1)
                act.wait_ge(bn_ready, 2 * j + 1)
                for bp in range(BP):
                    z = rows(Z0, REG, bp, 0, G)
                    nc.scalar.activation(z, z, ACT.Relu, bias=small[:, 13:14],
                                         scale=small[:, 12:13]).then_inc(relu_done, 1)
                square(2)
                square(3)
                act.wait_ge(table_done, j + 1)
                for k in range(BP + 4):
                    for q in range(Q):
                        if 0 <= k - 4 < BP:
                            c = (k - 4) * Q + q
                            n = LAY["invW", c]
                            if c == 0:
                                act.wait_ge(bn_ready, 2 * j + 2)
                            bk.full(n)
                            nc.scalar.activation(rows(X0, REG, k - 4, CH * q, CH), by_row(bank(n)), ACT.Identity,
                                                 bias=small[:, 13:14], scale=small[:, 12:13]).then_inc(drained[n % BANKS], 1)
                    for q in range(Q):
                        if 0 <= k - 3 < BP:
                            n = LAY["invH", (k - 3) * Q + q]
                            bk.full(n)
                            dst = backw[:, :].rearrange("p (h c) -> p c h", c=C)[:, 8 * q:8 * q + 8, :]
                            nc.scalar.activation(dst, by_channel(bank(n)), ACT.Identity).then_inc(drained[n % BANKS], 1)
                    for q in range(Q):
                        if 0 <= k < BP:
                            n = LAY["turn", k * Q + q]
                            bk.full(n)
                            dst = turned[:, :].rearrange("p (c h) -> p h c", h=H)[:, 16 * q:16 * q + 16, :]
                            nc.scalar.activation(dst, bank(n).rearrange("p (h c) -> p h c", c=C),
                                                 ACT.Identity).then_inc(drained[n % BANKS], 1)
                    if k == 2:
                        root(2)
            bk = Bank(act, PRO_ROUNDS + LAY_ROUNDS * (DEPTH - 1))
            for bp in range(BP):
                for q in range(Q):
                    bk.result(LAY["invW", Q * bp + q])
                nc.scalar.activation(planar(bp), interleaved(X0, bp), ACT.Identity).then_inc(unlaid, 1)

        @block.vector
        def _(dve):
            count = [0, 0]

            def link(ins):
                ins.then_inc(link_s, 1)
                count[0] += 1
                dve.wait_ge(link_s, count[1] + count[0])

            def prepare(layer):
                if isinstance(layer, int):
                    dve.wait_ge(consts_in, 16 * 6)
                dve.wait_ge(par_in, 16 * (layer + 1))
                link(nc.vector.tensor_reduce(ksum[:, :], parS[:, P_K:P_F].rearrange("p (k t o) -> p k o t", k=2, t=TAPS),
                                             op=ALU.add, axis=AX))
                for k in range(2):
                    for form in range(2):
                        o = (2 * k + form) * 3 * C
                        w = wts[:, o:o + 3 * C].rearrange("p (d o) -> p d o", o=C)
                        m = ksum[:, C * k:C * k + C].unsqueeze(1).broadcast_to([128, 3, C])
                        f = parS[:, P_F + o:P_F + o + 3 * C].rearrange("p (d o) -> p d o", o=C)
                        nc.vector.scalar_tensor_tensor(w, in0=m, scalar=cstS[:, C_MASK + form:C_MASK + form + 1], in1=f,
                                                       op0=ALU.mult, op1=ALU.add)
                nc.vector.tensor_copy(small[:, 14:16], parS[:, P_GB:P_GB + 2])
                ml = lsum[:, 0:16]
                row = lsum[:, 16:64].rearrange("p (c t) -> p c t", t=3)
                al, be = lsum[:, 64:80], lsum[:, 80:96]
                link(nc.vector.tensor_reduce(ml, parS[0:12, P_L9:P_ALL].rearrange("p (c t) -> p c t", t=TAPS),
                                             op=ALU.add, axis=AX))
                link(nc.vector.scalar_tensor_tensor(row, in0=ml.unsqueeze(2).broadcast_to([12, 16, 3]), scalar=-1.0 / TAPS,
                                                    in1=parS[0:12, P_L:P_L9].rearrange("p (c t) -> p c t", t=3),
                                                    op0=ALU.mult, op1=ALU.add))
                nc.vector.tensor_scalar(al, row[:, :, 1], cstS[0:12, C_ONE:C_ONE + 1], None, ALU.mult)
                link(nc.vector.scalar_tensor_tensor(be, in0=row[:, :, 0], scalar=cstS[0:12, C_SGN:C_SGN + 1],
                                                    in1=row[:, :, 2], op0=ALU.mult, op1=ALU.add))
                t3 = taps[:, :].rearrange("p (c k) -> p c k", k=64)
                link(nc.vector.tensor_tensor(t3, be.unsqueeze(2).broadcast_to([12, 16, 64]),
                                             cstS[0:12, C_CS:C_CS + 64].unsqueeze(1).broadcast_to([12, 16, 64]),
                                             op=ALU.mult))
                nc.vector.tensor_tensor(t3, t3, al.unsqueeze(2).broadcast_to([12, 16, 64]), op=ALU.add)\
                    .then_inc(prep_done, 1)
                dve.wait_ge(prep_done, layer + 1)

            for t in (X0, Z0):
                v = t[:, :].rearrange("p (b s) -> p b s", s=REG)
                nc.vector.memset(v[:, :, 0:G * GROUP].rearrange("p b (r w) -> p b r w", w=GROUP)[:, :, :, 0:2], 0.0)
                nc.vector.memset(v[:, :, G * GROUP:REG], 0.0)
            v = Z0[3 * C:128, :].rearrange("p (b s) -> p b s", s=REG)
            nc.vector.memset(v[:, :, (G - 1) * GROUP + 2:G * GROUP], 0.0)
            v = X2[:, :].rearrange("p (b s) -> p b s", s=REG2)
            nc.vector.memset(v[0:2 * C, :, 0:GROUP], 0.0)
            for t in (X2, Z2):
                v = t[:, :].rearrange("p (b s) -> p b s", s=REG2)
                last = nc.vector.memset(v[:, :, G * GROUP:REG2], 0.0)
            last.then_inc(zeroed, 1)

            bk = Bank(dve, 0)

            z3 = lgt.rearrange("p (s k) -> p s k", k=TAPS)
            e3 = ex.rearrange("p (s k) -> p s k", k=TAPS)
            q3 = pr.rearrange("p (s k) -> p s k", k=TAPS)
            part = p3.rearrange("p (g s m) -> p g s m", s=3, m=36)
            p4, r4 = (a.rearrange("p (g m) -> p g m", m=36) for a in (pr, rs))

            def leaky(bp, q):
                bk.result(PRO["conv", bp, q])
                u = hid[:, N * q:N * q + N]
                nc.vector.scalar_tensor_tensor(u, in0=u, scalar=LEAK, in1=u, op0=ALU.mult,
                                               op1=ALU.max).then_inc(hid_ready, 1)

            def less_max(bp, i):
                n = PRO["logits", bp, i]
                s = slice(32 * i, 32 * i + 32)
                bk.full(n)
                z = bank(n)[:, 0:288].rearrange("p (s k) -> p s k", k=TAPS)
                link(nc.vector.tensor_reduce(mx[:, s], z, op=ALU.max, axis=AX))
                nc.vector.tensor_tensor(z3[:, s], z, mx[:, s].unsqueeze(2).broadcast_to([128, 32, TAPS]),
                                        op=ALU.subtract).then_inc(drained[n % BANKS], 1)

            def probabilities(bp, i):
                s, g = slice(32 * i, 32 * i + 32), slice(8 * i, 8 * i + 8)
                dve.wait_ge(exp_out, 2 * bp + i + 1)
                link(nc.vector.tensor_reduce(sm[:, s], e3[:, s], op=ALU.add, axis=AX))
                link(nc.vector.reciprocal(rc[:, s], sm[:, s]))
                link(nc.vector.tensor_tensor(q3[:, s], e3[:, s], rc[:, s].unsqueeze(2).broadcast_to([128, 32, TAPS]),
                                             op=ALU.mult))
                if bp:
                    bk.full(PRO["probsT", bp - 1, 2 * i + 1])
                link(nc.vector.tensor_copy(part[:, g, 0], p4[:, g]))
                link(nc.vector.tensor_tensor(r4[:, g], p4[:, g], part[:, g, 0], op=ALU.subtract))
                link(nc.vector.tensor_copy(part[:, g, 1], r4[:, g]))
                link(nc.vector.tensor_tensor(r4[:, g], r4[:, g], part[:, g, 1], op=ALU.subtract))
                nc.vector.tensor_copy(part[:, g, 2], r4[:, g]).then_inc(probs_ready, 1)

            def two_x_less(c):
                n = PRO["sum", c]
                bk.full(n)
                if c:
                    dve.wait_ge(x_first, c)
                nc.vector.scalar_tensor_tensor(by_row(two_x_slot), in0=rows(X0, REG, c // Q, CH * (c % Q), CH), scalar=2.0,
                                               in1=by_row(bank(n)), op0=ALU.mult, op1=ALU.subtract)\
                    .then_inc(drained[n % BANKS], 1)

            for q in range(Q):
                leaky(0, q)
                if q % 2:
                    less_max(0, q // 2)
            probabilities(0, 0)
            for bp in range(BP):
                dve.wait_ge(shifted[bp], 16 * 4)
                for q in range(Q):
                    c = bp * Q + q
                    for k in range(TAPS):
                        if k == SUM_AT and c:
                            two_x_less(c - 1)
                        di, dj = k // 3, k % 3
                        src = (rows(Z2, REG2, bp, CH * q, CH, dj - 1), rows(X0, REG, bp, CH * q, CH, dj - 1),
                               rows(Z0, REG, bp, CH * q, CH, dj - 1))[di]
                        n = PRO["spread", bp, q, k]
                        bk.full(n)
                        if k in POOL_TAPS:
                            m = NP * c + POOL_TAPS.index(k)
                            if m >= 4:
                                dve.wait_ge(pool_sums, (NP - 1) * ((m - 4) // NP) + max((m - 4) % NP, 1))
                            dst = pool_slot[m % 4]
                        else:
                            dst = pe_slot[3 * (c % 2) + PE_TAPS.index(k)]
                        nc.vector.tensor_tensor(by_row(dst), src, by_row(bank(n)), op=ALU.mult)\
                            .then_inc(drained[n % BANKS], 1)
                        if k == 1 and q > 0 and bp + 1 < BP:
                            leaky(bp + 1, q - 1)
                        if k == 1 and q == 0 and bp > 0:
                            leaky(bp, 3)
                        if k == 4 and q == 1:
                            probabilities(bp, 1)
                        if k == 4 and q == 3 and bp + 1 < BP:
                            probabilities(bp + 1, 0)
                    if q == 2 and bp + 1 < BP:
                        less_max(bp + 1, 0)
                    if q == 0 and bp > 0:
                        less_max(bp, 1)
            prepare(0)
            two_x_less(NCH - 1)

            with dve.Fori(0, DEPTH) as j:
                assert count[0] == PRO_LINKS, count
                count[0], count[1] = 0, PRO_LINKS + LAY_LINKS * j
                bk = Bank(dve, PRO_ROUNDS + LAY_ROUNDS * j)
                S = lambda i: small[:, i:i + 1]

                def aggregate():
                    nc.vector.tensor_copy(S(16), S(14))
                    nc.vector.bn_aggr(small[:, 0:2], stats[:, :]).then_inc(mean_in, 1)

                def spread_of_means(which):
                    n = LAY["mean", which]
                    bk.full(n)
                    nc.vector.tensor_copy(S(2), bank(n)[:, 0:1]).then_inc(drained[n % BANKS], 1)
                    bk.result(n)
                    link(nc.vector.tensor_tensor(S(3), S(0), S(2), op=ALU.subtract))
                    nc.vector.scalar_tensor_tensor(S(4), in0=S(3), scalar=S(3), in1=S(1), op0=ALU.mult,
                                                   op1=ALU.add).then_inc(var_in, 1)

                def variance(which):
                    n = LAY["var", which]
                    bk.full(n)
                    nc.vector.tensor_scalar(S(7), bank(n)[:, 0:1], BN_EPS, None, ALU.add).then_inc(drained[n % BANKS], 1)

                def scale_and_bias(which):
                    dve.wait_ge(std_ready, 2 * j + which)
                    link(nc.vector.reciprocal(S(9), S(8)))
                    link(nc.vector.tensor_tensor(S(10), S(9), S(9), op=ALU.mult))
                    link(nc.vector.tensor_tensor(S(10), S(10), S(7), op=ALU.mult))
                    link(nc.vector.tensor_scalar(S(10), S(10), -0.5, 1.5, ALU.mult, ALU.add))
                    link(nc.vector.tensor_tensor(S(9), S(9), S(10), op=ALU.mult))
                    link(nc.vector.tensor_tensor(S(12), S(9), S(14), op=ALU.mult))
                    link(nc.vector.tensor_tensor(S(11), S(2), S(12), op=ALU.mult))
                    nc.vector.tensor_tensor(S(13), S(15), S(11), op=ALU.subtract).then_inc(bn_ready, 1)

                for c in range(NCH):
                    bk.result(LAY["conv1", c])
                    ins = nc.vector.bn_stats(stats[:, 6 * c:6 * c + 6], rows(Z0, REG, c // Q, CH * (c % Q), CH))
                link(ins)
                aggregate()
                spread_of_means(1)
                variance(1)
                scale_and_bias(1)

                for i in range(4):
                    bk.result(LAY["table", i])
                half = freqw[:, 0:1024]
                link(nc.vector.tensor_tensor(half, turned[:, 0:1024], turned[:, 1024:2048], op=ALU.add))
                link(nc.vector.tensor_scalar(half, half, 2 * STEP, 2.0, ALU.mult, ALU.add))
                link(nc.vector.reciprocal(half, half))
                h3 = half.rearrange("p (c k) -> p c k", k=64)
                a3, d3 = (t[:, :].rearrange("p (c k) -> p c k", k=64) for t in (tabA, tabD))
                nc.vector.tensor_tensor(a3, h3, h3[:, :, ::-1], op=ALU.add)
                link(nc.vector.tensor_tensor(d3, h3[:, :, ::-1], h3, op=ALU.subtract))
                nc.vector.tensor_scalar(a3[:, :, 0:64:63], h3[:, :, 0:64:63], 2.0, None, ALU.mult)
                nc.vector.tensor_scalar(d3[:, :, 0:64:63], d3[:, :, 0:64:63], 0.0, None, ALU.mult).then_inc(table_done, 1)
                dve.wait_ge(table_done, j + 1)

                for c in range(NCH):
                    n = LAY["conv2", c]
                    bk.full(n)
                    xc = rows(X0, REG, c // Q, CH * (c % Q), CH)
                    nc.vector.scalar_tensor_tensor(xc, in0=by_row(bank(n)), scalar=STEP, in1=xc, op0=ALU.mult,
                                                   op1=ALU.add).then_inc(drained[n % BANKS], 1)
                    bk.result(n)
                    ins = nc.vector.bn_stats(stats[:, 6 * c:6 * c + 6], xc)
                link(ins)
                aggregate()
                for k in range(BP + 4):
                    for q in range(Q):
                        if 0 <= k - 2 < BP:
                            n = LAY["fwdH", (k - 2) * Q + q]
                            bk.full(n)
                            src = bank(n).rearrange("p (c b k) -> p c b k", c=4, b=2)
                            for t, dst in ((tabA, specA), (tabD, specD)):
                                tt = t[:, 256 * q:256 * q + 256].rearrange("p (c k) -> p c k", k=64)\
                                    .unsqueeze(2).broadcast_to([128, 4, 2, 64])
                                to = dst[:, N * q:N * q + N].rearrange("p (c b k) -> p c b k", c=4, b=2)
                                if dst is specD:
                                    to = to[:, :, :, ::-1]
                                ins = nc.vector.tensor_tensor(to, src, tt, op=ALU.mult)
                            ins.then_inc(drained[n % BANKS], 1)
                    for q in range(Q):
                        if 0 <= k - 1 < BP:
                            n = LAY["fwdW", (k - 1) * Q + q]
                            bk.full(n)
                            nc.vector.tensor_copy(freqw[:, N * q:N * q + N], bank(n)).then_inc(drained[n % BANKS], 1)
                    if k == 1:
                        spread_of_means(2)
                    if k == 2:
                        variance(2)
                    if k == 3:
                        scale_and_bias(2)
                        prepare(j + 1)
                assert count[0] == LAY_LINKS, count

        @block.tensor
        def _(pe):
            def conv(bk, n, c, X, X2_, weights, form_stride):
                bp, q = divmod(c, Q)
                bk.claim(n)
                out_b = bank(n)
                for dj in range(3):
                    for r in range(R):
                        form, src, g = ((1, X2_, CH * q), (0, X, CH * q), (1, X, CH * q), (0, X2_, CH * q + 1))[r]
                        reg = REG2 if r in (0, 3) else REG
                        o = form * form_stride + dj * C
                        last = nc.tensor.matmul(out_b[C * r:C * r + C, :], weights[:, o:o + C],
                                                rows(src, reg, bp, g, CH, dj - 1), start=(dj == 0), stop=(dj == 2),
                                                tile_position=(0, C * r))
                last.then_inc(filled[n % BANKS], 1)

            bk = Bank(pe, 0)
            pe.wait_ge(consts_in, 16 * 6)
            pe.wait_ge(zeroed, 1)

            def hidden_conv(bp, q):
                if q == 0:
                    pe.wait_ge(x2_in[bp], 32)
                conv(bk, PRO["conv", bp, q], bp * Q + q, X0, X2, w1S, 3 * C)

            def logits(bp, i):
                n = PRO["logits", bp, i]
                bk.claim(n)
                pe.wait_ge(hid_ready, Q * bp + 2 * i + 2)
                for g in range(8):
                    p = (8 * i + g) * 128
                    last = nc.tensor.matmul(bank(n)[:, 36 * g:36 * g + 36], hid[:, p:p + 128], w2S[:, :],
                                            start=True, stop=True)
                last.then_inc(filled[n % BANKS], 1)

            def turn_probs(bp, q):
                n = PRO["probsT", bp, q]
                bk.claim(n)
                pe.wait_ge(probs_ready, 2 * bp + q // 2 + 1)
                for g in range(CH):
                    p = (CH * q + g) * 108
                    last = nc.tensor.transpose(bank(n).bitcast(bf16)[0:108, 128 * g:128 * g + 128], p3[:, p:p + 108],
                                               idbS[:, :])
                last.then_inc(filled[n % BANKS], 1)

            def add_up(c):
                n = PRO["sum", c]
                bk.claim(n)
                for k in PE_TAPS:
                    bk.result(PRO["spread", c // Q, c % Q, k])
                for i in range(len(PE_TAPS)):
                    last = nc.tensor.matmul(bank(n), cm(C_ID), pe_slot[3 * (c % 2) + i], start=(i == 0), stop=(i == len(PE_TAPS) - 1))
                last.then_inc(filled[n % BANKS], 1)

            for q in range(Q):
                hidden_conv(0, q)
                if q % 2:
                    logits(0, q // 2)
            turn_probs(0, 0)
            turn_probs(0, 1)
            for bp in range(BP):
                for q in range(Q):
                    bk.result(PRO["probsT", bp, q])
                    for k in range(TAPS):
                        if k == SUM_AT:
                            if bp * Q + q > 0:
                                add_up(bp * Q + q - 1)
                            if q == 2 and bp + 1 < BP:
                                logits(bp + 1, 0)
                            if q == 0 and bp > 0:
                                logits(bp, 1)
                        n = PRO["spread", bp, q, k]
                        bk.claim(n)
                        nc.tensor.matmul(bank(n), selS[:, 128 * k:128 * k + 128], pT[0:108, N * q:N * q + N],
                                         start=True, stop=True).then_inc(filled[n % BANKS], 1)
                    if q == 1:
                        turn_probs(bp, 2)
                        turn_probs(bp, 3)
                    if bp + 1 < BP:
                        if q == 3:
                            turn_probs(bp + 1, 0)
                            turn_probs(bp + 1, 1)
                        hidden_conv(bp + 1, q)
            add_up(NCH - 1)

            with pe.Fori(0, DEPTH) as j:
                bk = Bank(pe, PRO_ROUNDS + LAY_ROUNDS * j)
                pe.wait_ge(prep_done, j + 1)
                for c in range(NCH):
                    if c % Q == 0:
                        pe.wait_ge(x2_in[c // Q], 32 * (j + 2))
                    conv(bk, LAY["conv1", c], c, X0, X2, wts, 3 * C)

                def table(i):
                    n = LAY["table", i]
                    bk.claim(n)
                    e = (C_ERE, C_EIM)[i // 2]
                    nc.tensor.matmul(bank(n), cm(e, k=12), taps[:, N * (i % 2):N * (i % 2) + N], start=True,
                                     stop=True).then_inc(filled[n % BANKS], 1)

                def average(what, which, sem_, col):
                    n = LAY[what, which]
                    bk.claim(n)
                    pe.wait_ge(sem_, 2 * j + which)
                    nc.tensor.matmul(bank(n)[:, 0:1], cm(C_AVG), small[:, col:col + 1], start=True,
                                     stop=True).then_inc(filled[n % BANKS], 1)

                table(0)
                average("mean", 1, mean_in, 0)
                table(1)
                average("var", 1, var_in, 4)
                table(2)
                table(3)
                pe.wait_ge(edges, 1)
                for c in range(NCH):
                    if c % Q == 0:
                        pe.wait_ge(relu_done, BP * j + c // Q + 1)
                        pe.wait_ge(z2_in[c // Q], 32 * (j + 1))
                    conv(bk, LAY["conv2", c], c, Z0, Z2, wts[:, 2 * 3 * C:], 3 * C)
                for k in range(BP + 4):
                    for q in range(Q):
                        if 0 <= k - 4 < BP:
                            c = (k - 4) * Q + q
                            n = LAY["invW", c]
                            bk.claim(n)
                            for i in range(Q):
                                bk.result(LAY["invH", (k - 4) * Q + i])
                            for g in range(CH):
                                p = (CH * q + g) * 128
                                last = nc.tensor.matmul(bank(n)[:, 128 * g:128 * g + 128], backw[:, p:p + 128], cm(C_IW),
                                                        start=True, stop=True)
                            last.then_inc(filled[n % BANKS], 1)
                    for q in range(Q):
                        if 0 <= k - 3 < BP:
                            c = (k - 3) * Q + q
                            n = LAY["invH", c]
                            bk.claim(n)
                            bk.result(LAY["fwdH", c])
                            for cp in range(4):
                                p = N * q + 128 * cp
                                o = bank(n)[:, 128 * cp:128 * cp + 128]
                                nc.tensor.matmul(o, specA[:, p:p + 128], cm(C_FH), start=True, stop=False)
                                last = nc.tensor.matmul(o, specD[:, p:p + 128], cm(C_IR), start=False, stop=True)
                            last.then_inc(filled[n % BANKS], 1)
                    for q in range(Q):
                        if 0 <= k - 2 < BP:
                            c = (k - 2) * Q + q
                            n = LAY["fwdH", c]
                            bk.claim(n)
                            bk.result(LAY["fwdW", c])
                            nc.tensor.matmul(bank(n), cm(C_FH), freqw[:, N * q:N * q + N], start=True,
                                             stop=True).then_inc(filled[n % BANKS], 1)
                    for q in range(Q):
                        if 0 <= k - 1 < BP:
                            c = (k - 1) * Q + q
                            n = LAY["fwdW", c]
                            bk.claim(n)
                            for i in range(Q):
                                bk.result(LAY["turn", (k - 1) * Q + i])
                            for i in range(4):
                                p = (4 * q + i) * 128
                                last = nc.tensor.matmul(bank(n)[:, 128 * i:128 * i + 128], turned[:, p:p + 128],
                                                        cm(C_FW), start=True, stop=True)
                            last.then_inc(filled[n % BANKS], 1)
                    for q in range(Q):
                        if 0 <= k < BP:
                            c = k * Q + q
                            n = LAY["turn", c]
                            bk.claim(n)
                            bk.result(LAY["conv2", c])
                            for g in range(CH):
                                last = nc.tensor.transpose(bank(n)[:, 128 * g:128 * g + 128],
                                                           rows(X0, REG, k, CH * q + g, 1)[:, 0], cm(C_ID))
                            last.then_inc(filled[n % BANKS], 1)
                    if k == 1:
                        average("mean", 2, mean_in, 0)
                    if k == 2:
                        average("var", 2, var_in, 4)


def constants():
    n = np.arange(64)
    th = 2 * np.pi / 64
    freq = np.array([p if p <= 31 else (p - 63 if p < 63 else 32) for p in range(64)])

    def cas(a):
        return (np.cos(a) + np.sin(a)) / 8

    c = np.zeros((128, C_ALL), np.float64)
    two = np.eye(2)
    c[:, C_ID:C_ID + 128] = np.eye(128)
    fw = cas(th * np.outer(n, freq))
    c[:, C_FW:C_FW + 128] = np.kron(two, fw).reshape(2, 64, 128).transpose(1, 0, 2).reshape(128, 128)
    c[:, C_FH:C_FH + 128] = np.kron(two, cas(th * np.outer(n, n)))
    c[:, C_IR:C_IR + 128] = np.kron(two, cas(-th * np.outer(n, n)))
    c[:, C_IW:C_IW + 128] = c[:, C_FW:C_FW + 128].T
    c[:, C_AVG:C_AVG + 128] = np.kron(np.ones((R, R)), np.eye(C)) / R
    for c2 in range(2):
        for i in range(3):
            q = c2 * 6 + i * 2
            a = th * n * (i - 1)
            s = slice(64 * c2, 64 * c2 + 64)
            c[q, C_ERE:C_ERE + 128][s], c[q + 1, C_ERE:C_ERE + 128][s] = np.cos(a), -np.sin(a)
            c[q, C_EIM:C_EIM + 128][s], c[q + 1, C_EIM:C_EIM + 128][s] = np.sin(a), np.cos(a)
            c[q, C_CS:C_CS + 64], c[q + 1, C_CS:C_CS + 64] = np.cos(th * freq), np.sin(th * freq)
            c[q, C_ONE] = 1
            c[q, C_SGN], c[q + 1, C_SGN] = 1, -1
    for form in range(2):
        c[C * form:C * (form + 3), C_MASK + form] = -1.0 / TAPS
    sel = np.zeros((3, R, TAPS, TAPS, R, C), np.float32)
    for r in range(R):
        for k in range(TAPS):
            sel[:, r, k, k, r, :] = 1
    return c.astype(np.float32), sel.reshape(3 * R * TAPS, TAPS * 128), np.eye(128, dtype=np.float32)


def windows(k):
    o = np.zeros((R, k.shape[1], 2, 3, k.shape[3]), np.float32)
    for form in range(2):
        for di in range(3):
            o[di + form, :, form] = k[di]
    return o.reshape(128, -1)


def kernel(x, L0_conv_w1, L0_conv_b1, L0_conv_w2, L0_conv_b2, L1_conv_K, L1_conv_L, L1_conv_gamma, L1_conv_beta):
    import ml_dtypes
    import concourse.bacc as bacc
    from concourse.bass_utils import run_bass_kernel_spmd

    x, w1, b1, w2, b2, K, L, gamma, beta = (np.asarray(a) for a in (
        x, L0_conv_w1, L0_conv_b1, L0_conv_w2, L0_conv_b2, L1_conv_K, L1_conv_L, L1_conv_gamma, L1_conv_beta))
    cst, sel, idb = constants()
    par = np.zeros((DEPTH + 1, 128, P_ALL), np.float32)
    for j in range(DEPTH):
        for k, kern in enumerate((K[j].transpose(2, 1, 3, 0), K[j].transpose(2, 0, 3, 1)[::-1, :, ::-1])):
            flat = kern.transpose(1, 0, 2, 3).reshape(C, -1)
            for r in range(R):
                par[j, C * r:C * r + C, P_K + k * TAPS * C:P_K + (k + 1) * TAPS * C] = flat
            par[j, :, P_F + k * 6 * C:P_F + (k + 1) * 6 * C] = windows(kern)
        for r in range(R):
            par[j, C * r:C * r + C, P_GB] = gamma[j]
            par[j, C * r:C * r + C, P_GB + 1] = beta[j]
        for c2 in range(2):
            for i in range(3):
                for tr in range(2):
                    q = c2 * 6 + i * 2 + tr
                    par[j, q, P_L:P_L9] = L[j, c2::2, 0, i, :].reshape(-1)
                    par[j, q, P_L9:P_ALL] = L[j, c2::2, 0].reshape(-1)
    w1p = np.zeros((3, C, 3, C), np.float32)
    w1p[:, :, :, 0:HID] = w1.transpose(2, 1, 3, 0)
    b1p = np.zeros((R, C, 1), np.float32)
    b1p[:, 0:HID, 0] = b1
    b1p[:, HID, 0] = 1.0
    w2p = np.zeros((R, C, R, TAPS), np.float32)
    for r in range(R):
        w2p[r, 0:HID, r] = w2[:, :, 0, 0].T
        w2p[r, HID, r] = b2
    arrays = {
        "x": x, "par": par, "w1": windows(w1p), "b1": b1p.reshape(128, 1), "w2": w2p.reshape(128, R * TAPS),
        "cst": cst, "sel": sel.astype(ml_dtypes.bfloat16), "idb": idb.astype(ml_dtypes.bfloat16),
    }
    nc = bacc.Bacc("TRN2", target_bir_lowering=False, num_devices=1)
    args = [nc.dram_tensor(n, a.shape, mybir.dt.from_np(a.dtype), kind="ExternalInput").ap() for n, a in arrays.items()]
    out = nc.dram_tensor("out", (B, C, H, W), mybir.dt.float32, kind="ExternalOutput").ap()
    build(nc, *args, out)
    r = run_bass_kernel_spmd(nc, [arrays], core_ids=[0])
    return r.results[0]["out"]
```

```python
import numpy as np
import concourse.bass as bass
from concourse import mybir
from contextlib import ExitStack

B, C, H, W = 8, 32, 64, 64
R = 128 // C
G = H // R
BP = B // 2
TAPS = 9
HID = C // 2
DEPTH = 4
STEP = 0.1
BN_EPS = 1e-5
LEAK = 0.2

ROW = 2 * W
GROUP = ROW + 2
REG = G * GROUP + 4
REG2 = (G + 1) * GROUP + 4
CH = 4
Q = G // CH
NCH = BP * Q
N = CH * ROW
BANKS = 8
WORK = 2048
SL = W // 2

TURN_AT, FWDW_AT = NCH - 5, NCH - 3
SHARED = 2

C_ID, C_FW, C_FH, C_IH, C_IW, C_HH, C_HC, C_AVG, C_ERE, C_EIM = (128 * i for i in range(10))
C_CS = 10 * 128
C_ONE = C_CS + SL
C_SGN = C_ONE + 1
C_MASK = C_SGN + 1
C_ALL = C_MASK + 2
P_K = 0
P_F = P_K + 2 * TAPS * C
P_GB = P_F + 2 * 2 * 3 * C
P_L = P_GB + 2
P_L9 = P_L + C * 3
P_ALL = P_L9 + C * TAPS


def pe_taps(c):
    return (2, 5, 8) if c + 4 < NCH else (2, 4, 5, 8)


def pool_taps(c):
    return [k for k in range(TAPS) if k not in pe_taps(c)]


def pool_products(c):
    return sum(len(pool_taps(i)) for i in range(c))


def prologue_chunk(c):
    thirds = {}
    if c > 0:
        thirds.update({3 + i: ("sum", c - 1, i) for i in range(len(pe_taps(c - 1)))})
    elif 4 < NCH:
        thirds.update({3 + i: ("conv", 4, i) for i in range(3)})
    if c + 5 < NCH:
        thirds.update({6 + i: ("conv", c + 5, i) for i in range(3)})
    order = []
    for k in range(TAPS):
        order.append(("spread", c, k))
        if k in thirds:
            order.append(thirds[k])
    if c % 2 and c + 1 < NCH:
        order += [("probsT", c + 1), ("probsT", c + 2)]
        if c + 3 < NCH:
            order.append(("logits", (c + 3) // 2))
    return order


def prologue_schedule():
    order = [("conv", 0), ("conv", 1), ("logits", 0), ("conv", 2), ("conv", 3), ("logits", 1), ("probsT", 0), ("probsT", 1)]
    for c in range(NCH):
        order += [s[:2] if s[0] in ("sum", "conv") else s for s in prologue_chunk(c) if s[0] not in ("sum", "conv") or s[2] == 0]
    order.append(("sum", NCH - 1))
    return order


def inverse_stages(k):
    return (("invW", 4), ("invH", 3)) if k < BP + 2 else (("invH", 3), ("invW", 4))


def layer_schedule():
    order = [("conv1", c) for c in range(NCH)]
    order += [("table", 0), ("mean", 1), ("table", 1), ("var", 1), ("table", 2), ("table", 3)]
    for c in range(NCH):
        order.append(("conv2", c))
        if c == TURN_AT:
            order += [("turn", q) for q in range(Q)]
        if c == FWDW_AT:
            order += [("fwdW", q) for q in range(Q)]
    for k in range(1, BP + 4):
        for stage, lag in inverse_stages(k) + (("slot0", 2), ("fwdH", 2), ("fwdW", 1), ("slot0c", 2), ("turn", 0)):
            if 0 <= k - lag < BP and (stage, k) != ("fwdW", 1):
                order += [(stage, k - lag)] if stage in ("slot0", "slot0c") else [(stage, (k - lag) * Q + q) for q in range(Q)]
            if (stage, k) == ("fwdH", 2):
                order.append(("mean", 2))
        if k == 2:
            order.append(("var", 2))
    return order


PRO = {step: n for n, step in enumerate(prologue_schedule())}
LAY = {step: n for n, step in enumerate(layer_schedule())}
PRO_ROUNDS = len(PRO) // BANKS
LAY_ROUNDS = len(LAY) // BANKS
assert PRO_ROUNDS * BANKS == len(PRO) and LAY_ROUNDS * BANKS == len(LAY)
PRO_LINKS, LAY_LINKS = 29, 19


def build(nc, x_in, par, w1, b1, w2, cst, sel, idb, out):
    f32, bf16 = mybir.dt.float32, mybir.dt.bfloat16
    ALU, ACT, AX = mybir.AluOpType, mybir.ActivationFunctionType, mybir.AxisListType.X

    with ExitStack() as ctx:
        def sb(name, cols, dt=f32, parts=128):
            return ctx.enter_context(nc.sbuf_tensor(name, [parts, cols], dt))

        def sem(name):
            return ctx.enter_context(nc.semaphore(name))

        X0 = sb("X0", BP * REG)
        X2 = sb("X2", BP * REG2)
        Z0 = sb("Z0", BP * REG)
        Z2 = sb("Z2", BP * REG2)
        work = [sb(f"work{i}", WORK) for i in range(5)]
        turned, freqw, spec, rest, backw0 = work
        taps = rest[0:12, 0:C * SL]
        slot0 = rest[:, C * SL:C * SL + 2 * C]
        tabT = sb("tabT", C * SL)
        spare = sb("spare", 5 * N)
        parS = sb("parS", P_ALL)
        cstS = sb("cstS", C_ALL)
        wts = sb("wts", 2 * 2 * 3 * C)
        w1S = sb("w1S", 3 * 3 * C)
        w2S = sb("w2S", R * TAPS, parts=3 * C)
        b1S = sb("b1S", 1, parts=3 * C)
        selS = sb("selS", TAPS * 128, bf16, parts=3 * R * TAPS)
        idbS = sb("idbS", 128, bf16)
        stats = sb("stats", NCH * 6)
        small = sb("small", 32)
        backw = (backw0, spare[:, 0:WORK])
        ksum = sb("ksum", 2 * C)
        lsum = sb("lsum", 6 * C, parts=12)
        psum = ctx.enter_context(nc.psum_tensor("psum", [128, BANKS, N], f32))

        def cm(c, n=128, k=128):
            return cstS[0:k, c:c + n]

        def rows(t, reg, bp, g, n, shift=0, p0=0, p1=128):
            o = bp * reg + g * GROUP + 2 + 2 * shift
            return t[p0:p1, o:o + n * GROUP].rearrange("p (r w) -> p r w", w=GROUP)[:, :, 0:ROW]

        def bank(n):
            return psum[:, n % BANKS, :]

        filled = [sem(f"bank_filled{i}") for i in range(BANKS)]
        drained = [sem(f"bank_drained{i}") for i in range(BANKS)]
        consts_in = sem("consts_in")
        par_in = sem("par_in")
        zeroed = sem("zeroed")
        x_in_sem = [sem(f"x_loaded{i}") for i in range(BP)]
        shifted = [sem(f"shifted{i}") for i in range(BP)]
        x2_in = [sem(f"x2_in{i}") for i in range(BP)]
        z2_in = [sem(f"z2_in{i}") for i in range(BP)]
        relaid = sem("relaid")
        edge_zeros = sem("edge_zeros")
        weights_ready = sem("weights_ready")
        prep_done = sem("prep_done")
        hid_ready = sem("hid_ready")
        exp_out = sem("exp_out")
        to_cut = sem("to_cut")
        parts_cut = sem("parts_cut")
        pool_sums = sem("pool_sums")
        x_first = sem("x_first")
        edges = sem("edges")
        link_s = sem("dve_link")
        mean_in = sem("mean_in")
        var_in = sem("var_in")
        std_ready = sem("std_ready")
        bn_ready = sem("bn_ready")
        relu_done = sem("relu_done")
        table_done = sem("table_done")
        out_done = sem("out_done")

        hid = work[0]
        lgt, ex = work[1][:, 0:576], work[1][:, 576:1152]
        mx, sm, rc = (work[1][:, 1152 + 64 * i:1216 + 64 * i] for i in range(3))
        pr, rs = work[2][:, 0:576], work[2][:, 576:1152]
        accP = [work[2][:, 1152:1152 + N], work[1][:, 1344:1344 + N]]
        p3 = work[3][:, 0:864].bitcast(bf16)
        part = p3.rearrange("p (g s m) -> p g s m", s=3, m=36)
        p4, r4 = (a.rearrange("p (g m) -> p g m", m=36) for a in (pr, rs))
        pT = work[3][:, 1024:2048].bitcast(bf16)
        pool_slot = [work[4][:, N * i:N * (i + 1)] for i in range(4)]
        pe_slot = [tabT[:, 0:N], tabT[:, N:2 * N]] + [spare[:, N * i:N * i + N] for i in range(4)]
        two_x_slot = spare[:, 4 * N:5 * N]

        def pe_product(c, i):
            return pe_slot[3 * (c % 2) + i] if i < 3 else hid[:, N * (c % 2):N * (c % 2) + N]

        block = ctx.enter_context(nc.Block())

        class Bank:

            def __init__(self, eng, base):
                self.eng, self.base = eng, base

            def claim(self, n):
                if not isinstance(self.base, int) or self.base + n // BANKS > 0:
                    self.eng.wait_ge(drained[n % BANKS], self.base + n // BANKS)

            def full(self, n):
                self.eng.wait_ge(filled[n % BANKS], self.base + n // BANKS + 1)

            def result(self, n):
                self.eng.wait_ge(drained[n % BANKS], self.base + n // BANKS + 1)

        def made(bk, m, *later):
            if all(m % BANKS != n % BANKS for n in later):
                bk.result(m)

        def by_row(ap):
            return ap.rearrange("p (r w) -> p r w", w=ROW)

        def forth_from_w(n, q):
            src = bank(n).rearrange("p (c b t s) -> p t c b s", c=4, b=2, t=2)
            dst = freqw[:, N * q:N * q + N].rearrange("p (c e b s) -> p e c b s", c=4, e=2, b=2)
            return [(dst[64 * part:64 * part + 64, e], src[64 * e:64 * e + 64, part]) for e in range(2) for part in range(2)]

        def back_from_h(n, bp, q):
            src = bank(n).rearrange("p (c t h) -> p t c h", c=4, t=2)
            dst = backw[bp % 2][:, :].rearrange("p (h c e) -> p e c h", c=C // 2, e=2)[:, :, 4 * q:4 * q + 4]
            return [(dst[64 * part:64 * part + 64, e], src[64 * e:64 * e + 64, part]) for e in range(2) for part in range(2)]

        def planar(bp, r=None):
            p0, p1 = (0, 128) if r is None else (C * r, C * r + C)
            return Z2[p0:p1, bp * REG2:bp * REG2 + G * ROW].rearrange("p (g b w) -> p g b w", b=2, w=W)

        def interleaved(t, bp):
            return rows(t, REG, bp, 0, G).rearrange("p g (w b) -> p g b w", b=2)

        def in_dram(t, bp, b2, r):
            return t[2 * bp + b2].rearrange("c (g r) w -> r c g w", r=R)[r]

        def load_x(eng, bp, b2):
            for r in range(R):
                eng.dma_start(planar(bp, r)[:, :, b2], in_dram(x_in, bp, b2, r)).then_inc(x_in_sem[bp], 16)

        def shift_two(eng, dst, src, bp, done):
            s, d, n = bp * REG, bp * REG2, G * GROUP
            eng.dma_start(dst[0:2 * C, d + GROUP:d + GROUP + n], src[2 * C:128, s:s + n]).then_inc(done, 16)
            eng.dma_start(dst[2 * C:128, d:d + n], src[0:2 * C, s:s + n]).then_inc(done, 16)

        @block.sync
        def _(sp):
            load_x(sp, 0, 0)
            sp.dma_start(w1S[:, :], w1).then_inc(consts_in, 16)
            sp.dma_start(b1S[:, :], b1).then_inc(consts_in, 16)
            sp.dma_start(w2S[:, :], w2).then_inc(consts_in, 16)
            sp.dma_start(selS[:, :], sel).then_inc(consts_in, 16)
            sp.dma_start(idbS[:, :], idb).then_inc(consts_in, 16)
            sp.dma_start(cstS[:, :], cst).then_inc(consts_in, 16)
            sp.wait_ge(zeroed, 1)
            for bp in range(BP):
                sp.wait_ge(relaid, bp + 1)
                shift_two(sp, X2, X0, bp, x2_in[bp])
                s, n = bp * REG, G * GROUP
                m = bp * REG2
                sp.dma_start(Z0[0:3 * C, s:s + n], X0[C:128, s:s + n]).then_inc(shifted[bp], 16)
                sp.dma_start(Z0[3 * C:128, s:s + n - GROUP], X0[0:C, s + GROUP:s + n]).then_inc(shifted[bp], 16)
                sp.wait_ge(edge_zeros, bp + 1)
                sp.dma_start(Z2[C:128, m:m + n], X0[0:3 * C, s:s + n]).then_inc(shifted[bp], 16)
                sp.dma_start(Z2[0:C, m + GROUP:m + n], X0[3 * C:128, s:s + n - GROUP]).then_inc(shifted[bp], 16)
                if bp + 1 < BP:
                    load_x(sp, bp + 1, 0)
                    load_x(sp, bp + 1, 1)
                if bp == 0:
                    sp.dma_start(parS[:, :], par[0]).then_inc(par_in, 16)

            def layer(j, last=False):
                bk, before = Bank(sp, PRO_ROUNDS + LAY_ROUNDS * j), Bank(sp, PRO_ROUNDS + LAY_ROUNDS * (j - 1))
                for bp in range(BP):
                    sp.wait_ge(x_first, Q * bp + Q)
                    before.result(LAY["invW", Q * bp + Q - 1])
                    shift_two(sp, X2, X0, bp, x2_in[bp])
                if not last:
                    sp.wait_ge(prep_done, j + 1)
                    sp.dma_start(parS[:, :], par[bass.ds(j + 1, 1)].rearrange("o p c -> (o p) c")).then_inc(par_in, 16)
                for bp in range(BP):
                    bk.result(LAY["conv1", Q * bp + Q - 1])
                    shift_two(sp, Z2, Z0, bp, z2_in[bp])

            with sp.Fori(0, DEPTH - 1) as j:
                layer(j)
            layer(DEPTH - 1, last=True)
            bk = Bank(sp, PRO_ROUNDS + LAY_ROUNDS * (DEPTH - 1))
            for bp in range(BP):
                bk.result(LAY["invW", Q * bp + Q - 1])
                for b2 in range(2):
                    for r in range(R):
                        sp.dma_start(in_dram(out, bp, b2, r), planar(bp, r)[:, :, b2]).then_inc(out_done, 16)
            sp.wait_ge(out_done, 16 * B * R)

        @block.gpsimd
        def _(pool):
            def edge(bp):
                pool.wait_ge(relaid, bp + 1)
                nc.gpsimd.memset(Z2[0:2 * C, bp * REG2:bp * REG2 + GROUP], 0.0).then_inc(edge_zeros, 1)

            edge(0)
            edge(1)

            bk = Bank(pool, 0)

            def finish(c):
                if c < 0:
                    return
                pool.wait_ge(pool_sums, pool_products(c + 1) - (c + 1))
                bk.result(PRO["sum", c])
                nc.gpsimd.tensor_tensor(rows(X0, REG, c // Q, CH * (c % Q), CH), by_row(two_x_slot), by_row(accP[c % 2]),
                                        op=ALU.subtract).then_inc(x_first, 1)

            for c in range(NCH):
                bp, q = divmod(c, Q)
                if q == 2 and bp + 2 < BP:
                    edge(bp + 2)
                taps_, first = pool_taps(c), pool_products(c)
                for k in range(1, len(taps_)):
                    if k == 1:
                        bk.result(PRO["spread", c, 0])
                        if c >= 2:
                            pool.wait_ge(x_first, c - 1)
                        a = pool_slot[first % 4]
                    else:
                        pool.wait_ge(pool_sums, first - c + k - 1)
                        a = accP[c % 2]
                    bk.result(PRO["spread", c, taps_[k]])
                    nc.gpsimd.tensor_tensor(accP[c % 2], a, pool_slot[(first + k) % 4], op=ALU.add)\
                        .then_inc(pool_sums, 1)
                finish(c - 1)
            finish(NCH - 1)
            nc.gpsimd.memset(Z2[0:2 * C, :].rearrange("p (b s) -> p b s", s=REG2)[:, :, 0:GROUP], 0.0).then_inc(edges, 1)

        @block.scalar
        def _(act):
            load_x(act, 0, 1)
            bk = Bank(act, 0)

            def hidden(c):
                n = PRO["conv", c]
                bk.full(n)
                nc.scalar.activation(hid[0:3 * C, N * (c % Q):N * (c % Q) + N], bank(n)[0:3 * C, :], ACT.Identity,
                                     bias=b1S[:, 0:1]).then_inc(drained[n % BANKS], 1)

            def exps(h):
                o = 288 * (h % 2)
                bk.result(PRO["logits", h])
                nc.scalar.activation(ex[:, o:o + 288], lgt[:, o:o + 288], ACT.Exp).then_inc(exp_out, 1)

            def cut(h, i):
                act.wait_ge(to_cut, 3 * h + i + 1)
                if i == 0 and h > 1:
                    bk.full(PRO["probsT", 2 * h - 3])
                g = slice(8 * (h % 2), 8 * (h % 2) + 8)
                nc.scalar.activation(part[:, g, i], (r4 if i else p4)[:, g], ACT.Copy).then_inc(parts_cut, 1)

            def probs_turn(c):
                n = PRO["probsT", c]
                bk.full(n)
                nc.scalar.activation(pT[0:108, N * (c % Q):N * (c % Q) + N], bank(n).bitcast(bf16)[0:108, 0:N],
                                     ACT.Copy).then_inc(drained[n % BANKS], 1)

            def interleave(bp):
                act.wait_ge(x_in_sem[bp], 16 * 2 * R)
                nc.scalar.activation(interleaved(X0, bp), planar(bp), ACT.Identity).then_inc(relaid, 1)

            interleave(0)
            act.wait_ge(consts_in, 16 * 6)
            hidden(0)
            hidden(1)
            exps(0)
            hidden(2)
            hidden(3)
            interleave(1)
            for i in range(3):
                cut(0, i)
            probs_turn(0)
            probs_turn(1)
            for c in range(NCH):
                if c % 2 == 0 and c + 2 < NCH:
                    exps(c // 2 + 1)
                if c == 0:
                    hidden(4)
                if c % 2 and c + 1 < NCH:
                    cut((c + 1) // 2, 2)
                if c + 5 < NCH:
                    hidden(c + 5)
                if c % 2 == 0 and c + 2 < NCH:
                    cut(c // 2 + 1, 0)
                    cut(c // 2 + 1, 1)
                if c % 2 and c + 1 < NCH:
                    probs_turn(c + 1)
                    probs_turn(c + 2)
                if c % Q == 1 and c // Q + 2 < BP:
                    interleave(c // Q + 2)

            def layer(j, last_layer=False):
                bk = Bank(act, PRO_ROUNDS + LAY_ROUNDS * j)
                nc.scalar.activation(small[:, 20:21], cm(C_AVG, 1), ACT.Sqrt)
                for c in range(NCH):
                    n = LAY["conv1", c]
                    bk.full(n)
                    nc.scalar.activation(rows(Z0, REG, c // Q, CH * (c % Q), CH), by_row(bank(n)),
                                         ACT.Identity).then_inc(drained[n % BANKS], 1)

                def square(i):
                    n = LAY["table", i]
                    bk.full(n)
                    nc.scalar.activation(turned[:, N * i:N * i + N], bank(n), ACT.Square).then_inc(drained[n % BANKS], 1)

                def root(which):
                    bk.result(LAY["var", which])
                    nc.scalar.activation(small[:, 8:9], small[:, 7:8], ACT.Sqrt).then_inc(std_ready, 1)

                def norm_relu(bp, g, n):
                    parts = [(Z0, REG, g, n, 0, 128)]
                    if g == 0:
                        parts += [(Z2, REG2, 0, 1, 2 * C, 128), (Z2, REG2, 1, n, 0, 128)]
                    elif g + n < G:
                        parts += [(Z2, REG2, g + 1, n, 0, 128)]
                    else:
                        parts += [(Z2, REG2, g + 1, n - 1, 0, 128), (Z2, REG2, G, 1, 0, 2 * C)]
                    for t, reg, g, n, p0, p1 in parts:
                        z = rows(t, reg, bp, g, n, 0, p0, p1)
                        last = nc.scalar.activation(z, z, ACT.Relu, bias=small[p0:p1, 13:14], scale=small[p0:p1, 12:13])
                    last.then_inc(relu_done, 1)

                root(1)
                act.wait_ge(bn_ready, 2 * j + 1)
                for bp in range(BP):
                    act.wait_ge(z2_in[bp], 32 * (j + 1))
                    norm_relu(bp, 0, CH)
                    norm_relu(bp, CH, G - CH)
                    if bp == 0:
                        for i in range(4):
                            square(i)

                def keep_turned(bp, q):
                    n = LAY["turn", bp * Q + q]
                    bk.full(n)
                    dst = turned[:, :].rearrange("p (c h) -> p h c", h=H)[:, 16 * q:16 * q + 16, :]
                    nc.scalar.activation(dst, bank(n).rearrange("p (h c) -> p h c", c=C),
                                         ACT.Identity).then_inc(drained[n % BANKS], 1)

                def keep_fwdW(bp, q):
                    n = LAY["fwdW", bp * Q + q]
                    bk.full(n)
                    for dst, src in forth_from_w(n, q):
                        last = nc.scalar.activation(dst, src, ACT.Identity)
                    last.then_inc(drained[n % BANKS], 1)

                def keep_invH(bp, q):
                    n = LAY["invH", bp * Q + q]
                    bk.full(n)
                    for dst, src in back_from_h(n, bp, q):
                        last = nc.scalar.activation(dst, src, ACT.Identity)
                    last.then_inc(drained[n % BANKS], 1)

                def keep_invW(bp, q):
                    n = LAY["invW", bp * Q + q]
                    if bp * Q + q == 0:
                        act.wait_ge(bn_ready, 2 * j + 2)
                    bk.full(n)
                    if last_layer:
                        dst = planar(bp)[:, CH * q:CH * q + CH]
                        src = bank(n).rearrange("p (g w b) -> p g b w", g=CH, b=2)
                    else:
                        dst, src = rows(X0, REG, bp, CH * q, CH), by_row(bank(n))
                    nc.scalar.activation(dst, src, ACT.Identity, bias=small[:, 13:14],
                                         scale=small[:, 12:13]).then_inc(drained[n % BANKS], 1)

                act.wait_ge(table_done, j + 1)
                for q in range(Q):
                    keep_turned(0, q)
                for q in range(1, Q, 2):
                    keep_fwdW(0, q)
                for k in range(1, BP + 4):
                    for stage, lag in inverse_stages(k):
                        for q in range(0, Q, 2 if stage == "invH" and k - lag == BP - 1 else 1):
                            if 0 <= k - lag < BP:
                                (keep_invW if stage == "invW" else keep_invH)(k - lag, q)
                    for q in range(1, Q, 2):
                        if 1 <= k - 1 < SHARED:
                            keep_fwdW(k - 1, q)
                    if 0 <= k - 2 < BP:
                        n = LAY["slot0c", k - 2]
                        bk.full(n)
                        nc.scalar.activation(spec[:, :].rearrange("p (a s) -> p a s", s=SL)[:, :, 0], bank(n)[:, 0:2 * C],
                                             ACT.Identity).then_inc(drained[n % BANKS], 1)
                    for q in range(Q):
                        if 0 <= k < BP:
                            keep_turned(k, q)
                    if k == 2:
                        root(2)

            with act.Fori(0, DEPTH - 1) as j:
                layer(j)
            layer(DEPTH - 1, last_layer=True)

        @block.vector
        def _(dve):
            count = [0, 0]

            def link(ins):
                ins.then_inc(link_s, 1)
                count[0] += 1
                dve.wait_ge(link_s, count[1] + count[0])

            def prepare(layer):
                if isinstance(layer, int):
                    dve.wait_ge(consts_in, 16 * 6)
                dve.wait_ge(par_in, 16 * (layer + 1))
                link(nc.vector.tensor_reduce(ksum[:, :], parS[:, P_K:P_F].rearrange("p (k t o) -> p k o t", k=2, t=TAPS),
                                             op=ALU.add, axis=AX))
                for k in range(2):
                    for form in range(2):
                        o = (2 * k + form) * 3 * C
                        w = wts[:, o:o + 3 * C].rearrange("p (d o) -> p d o", o=C)
                        m = ksum[:, C * k:C * k + C].unsqueeze(1).broadcast_to([128, 3, C])
                        f = parS[:, P_F + o:P_F + o + 3 * C].rearrange("p (d o) -> p d o", o=C)
                        nc.vector.scalar_tensor_tensor(w, in0=m, scalar=cstS[:, C_MASK + form:C_MASK + form + 1], in1=f,
                                                       op0=ALU.mult, op1=ALU.add)
                nc.vector.tensor_copy(small[:, 14:16], parS[:, P_GB:P_GB + 2]).then_inc(weights_ready, 1)

            def prepare_taps(layer):
                ml = lsum[:, 0:C]
                row = lsum[:, C:4 * C].rearrange("p (c t) -> p c t", t=3)
                al, be = lsum[:, 4 * C:5 * C], lsum[:, 5 * C:6 * C]
                link(nc.vector.tensor_reduce(ml, parS[0:12, P_L9:P_ALL].rearrange("p (c t) -> p c t", t=TAPS),
                                             op=ALU.add, axis=AX))
                link(nc.vector.scalar_tensor_tensor(row, in0=ml.unsqueeze(2).broadcast_to([12, C, 3]), scalar=-1.0 / TAPS,
                                                    in1=parS[0:12, P_L:P_L9].rearrange("p (c t) -> p c t", t=3),
                                                    op0=ALU.mult, op1=ALU.add))
                nc.vector.tensor_scalar(al, row[:, :, 1], cstS[0:12, C_ONE:C_ONE + 1], None, ALU.mult)
                link(nc.vector.scalar_tensor_tensor(be, in0=row[:, :, 0], scalar=cstS[0:12, C_SGN:C_SGN + 1],
                                                    in1=row[:, :, 2], op0=ALU.mult, op1=ALU.add))
                t3 = taps[:, :].rearrange("p (c s) -> p c s", s=SL)
                link(nc.vector.tensor_tensor(t3, be.unsqueeze(2).broadcast_to([12, C, SL]),
                                             cstS[0:12, C_CS:C_CS + SL].unsqueeze(1).broadcast_to([12, C, SL]),
                                             op=ALU.mult))
                nc.vector.tensor_tensor(t3, t3, al.unsqueeze(2).broadcast_to([12, C, SL]), op=ALU.add)\
                    .then_inc(prep_done, 1)
                dve.wait_ge(prep_done, layer + 1)

            for t in (X0, Z0):
                v = t[:, :].rearrange("p (b s) -> p b s", s=REG)
                nc.vector.memset(v[:, :, 0:G * GROUP].rearrange("p b (r w) -> p b r w", w=GROUP)[:, :, :, 0:2], 0.0)
                nc.vector.memset(v[:, :, G * GROUP:REG], 0.0)
            v = Z0[3 * C:128, :].rearrange("p (b s) -> p b s", s=REG)
            nc.vector.memset(v[:, :, (G - 1) * GROUP + 2:G * GROUP], 0.0)
            v = X2[:, :].rearrange("p (b s) -> p b s", s=REG2)
            nc.vector.memset(v[0:2 * C, :, 0:GROUP], 0.0)
            for t in (X2, Z2):
                v = t[:, :].rearrange("p (b s) -> p b s", s=REG2)
                last = nc.vector.memset(v[:, :, G * GROUP:REG2], 0.0)
            last.then_inc(zeroed, 1)

            bk = Bank(dve, 0)

            z3 = lgt.rearrange("p (s k) -> p s k", k=TAPS)
            e3 = ex.rearrange("p (s k) -> p s k", k=TAPS)
            q3 = pr.rearrange("p (s k) -> p s k", k=TAPS)

            def leaky(c):
                bk.result(PRO["conv", c])
                u = hid[0:3 * C, N * (c % Q):N * (c % Q) + N]
                nc.vector.scalar_tensor_tensor(u, in0=u, scalar=LEAK, in1=u, op0=ALU.mult,
                                               op1=ALU.max).then_inc(hid_ready, 1)

            def step(ins):
                ins.then_inc(link_s, 1)
                count[0] += 1

            def less_max(h, i):
                n = PRO["logits", h]
                s = slice(32 * (h % 2), 32 * (h % 2) + 32)
                z = bank(n)[:, 0:288].rearrange("p (s k) -> p s k", k=TAPS)
                if i == 0:
                    bk.full(n)
                    step(nc.vector.tensor_reduce(mx[:, s], z, op=ALU.max, axis=AX))
                else:
                    dve.wait_ge(link_s, count[0])
                    nc.vector.tensor_tensor(z3[:, s], z, mx[:, s].unsqueeze(2).broadcast_to([128, 32, TAPS]),
                                            op=ALU.subtract).then_inc(drained[n % BANKS], 1)

            def probabilities(h, i):
                s, g = slice(32 * (h % 2), 32 * (h % 2) + 32), slice(8 * (h % 2), 8 * (h % 2) + 8)
                if i == 0:
                    dve.wait_ge(exp_out, h + 1)
                elif i < 3:
                    dve.wait_ge(link_s, count[0])
                else:
                    dve.wait_ge(parts_cut, 3 * h + i - 2)
                if i == 0:
                    step(nc.vector.tensor_reduce(sm[:, s], e3[:, s], op=ALU.add, axis=AX))
                elif i == 1:
                    step(nc.vector.reciprocal(rc[:, s], sm[:, s]))
                elif i == 2:
                    nc.vector.tensor_tensor(q3[:, s], e3[:, s], rc[:, s].unsqueeze(2).broadcast_to([128, 32, TAPS]),
                                            op=ALU.mult).then_inc(to_cut, 1)
                else:
                    before = p4 if i == 3 else r4
                    nc.vector.tensor_tensor(r4[:, g], before[:, g], part[:, g, i - 3], op=ALU.subtract).then_inc(to_cut, 1)

            def two_x_less(c):
                n = PRO["sum", c]
                bk.full(n)
                if c:
                    dve.wait_ge(x_first, c)
                nc.vector.scalar_tensor_tensor(by_row(two_x_slot), in0=rows(X0, REG, c // Q, CH * (c % Q), CH), scalar=2.0,
                                               in1=by_row(bank(n)), op0=ALU.mult, op1=ALU.subtract)\
                    .then_inc(drained[n % BANKS], 1)

            leaky(0)
            leaky(1)
            for i in range(2):
                less_max(0, i)
            leaky(2)
            leaky(3)
            for i in range(5):
                probabilities(0, i)
            for c in range(NCH):
                bp, q = divmod(c, Q)
                if q == 0:
                    dve.wait_ge(shifted[bp], 16 * 4)
                for k in range(TAPS):
                    di, dj = k // 3, k % 3
                    src = (rows(Z2, REG2, bp, CH * q, CH, dj - 1), rows(X0, REG, bp, CH * q, CH, dj - 1),
                           rows(Z0, REG, bp, CH * q, CH, dj - 1))[di]
                    n = PRO["spread", c, k]
                    bk.full(n)
                    if k in pool_taps(c):
                        m = pool_products(c) + pool_taps(c).index(k)
                        if m >= 4:
                            e = max(i for i in range(c + 1) if pool_products(i) <= m - 4)
                            dve.wait_ge(pool_sums, pool_products(e) - e + max(m - 4 - pool_products(e), 1))
                        dst = pool_slot[m % 4]
                    else:
                        dst = pe_product(c, pe_taps(c).index(k))
                    nc.vector.tensor_tensor(by_row(dst), src, by_row(bank(n)), op=ALU.mult)\
                        .then_inc(drained[n % BANKS], 1)
                    if k == 1 and 1 <= c and c + 4 < NCH:
                        leaky(c + 4 if c > 1 else 4)
                    if k == 3 and c == 1:
                        leaky(5)
                    if k == 5 and c > 0:
                        two_x_less(c - 1)
                    if c % 2 == 0 and c + 2 < NCH:
                        if k < 2:
                            less_max(c // 2 + 1, k)
                        if k in (4, 5, 6, 8):
                            probabilities(c // 2 + 1, min(k - 4, 3))
                    if c % 2 and c + 1 < NCH and k == 1:
                        probabilities((c + 1) // 2, 4)
            prepare(0)
            two_x_less(NCH - 1)
            prepare_taps(0)

            def layer(j, last_layer=False):
                count[0], count[1] = 0, PRO_LINKS + LAY_LINKS * j
                bk = Bank(dve, PRO_ROUNDS + LAY_ROUNDS * j)
                S = lambda i: small[:, i:i + 1]

                def aggregate():
                    nc.vector.tensor_copy(S(16), S(14))
                    nc.vector.bn_aggr(small[:, 0:2], stats[:, :]).then_inc(mean_in, 1)

                def spread_of_means(which):
                    n = LAY["mean", which]
                    bk.full(n)
                    nc.vector.tensor_copy(S(2), bank(n)[:, 0:1]).then_inc(drained[n % BANKS], 1)
                    bk.result(n)
                    nc.vector.tensor_scalar(S(11), S(2), -1.0, None, ALU.mult)
                    link(nc.vector.tensor_tensor(S(3), S(0), S(2), op=ALU.subtract))
                    nc.vector.scalar_tensor_tensor(S(4), in0=S(3), scalar=S(3), in1=S(1), op0=ALU.mult,
                                                   op1=ALU.add).then_inc(var_in, 1)

                def variance(which):
                    n = LAY["var", which]
                    bk.full(n)
                    nc.vector.tensor_scalar(S(7), bank(n)[:, 0:1], BN_EPS, None, ALU.add).then_inc(drained[n % BANKS], 1)

                def scale_and_bias(which):
                    dve.wait_ge(std_ready, 2 * j + which)
                    link(nc.vector.reciprocal(S(9), S(8)))
                    link(nc.vector.scalar_tensor_tensor(S(10), in0=S(9), scalar=S(9), in1=S(7), op0=ALU.mult, op1=ALU.mult))
                    link(nc.vector.tensor_scalar(S(10), S(10), -0.5, 1.5, ALU.mult, ALU.add))
                    link(nc.vector.scalar_tensor_tensor(S(12), in0=S(10), scalar=S(9), in1=S(14), op0=ALU.mult, op1=ALU.mult))
                    nc.vector.scalar_tensor_tensor(S(13), in0=S(11), scalar=S(12), in1=S(15), op0=ALU.mult,
                                                   op1=ALU.add).then_inc(bn_ready, 1)

                for c in range(NCH):
                    bk.result(LAY["conv1", c])
                    ins = nc.vector.bn_stats(stats[:, 6 * c:6 * c + 6], rows(Z0, REG, c // Q, CH * (c % Q), CH))
                link(ins)
                aggregate()
                spread_of_means(1)
                variance(1)
                scale_and_bias(1)

                for i in range(4):
                    bk.result(LAY["table", i])
                link(nc.vector.tensor_tensor(tabT[:, :], turned[:, 0:1024], turned[:, 1024:2048], op=ALU.add))
                link(nc.vector.tensor_scalar(tabT[:, :], tabT[:, :], STEP, 1.0, ALU.mult, ALU.add))
                nc.vector.reciprocal(tabT[:, :], tabT[:, :]).then_inc(table_done, 1)
                dve.wait_ge(table_done, j + 1)

                def keep_fwdW(bp, q):
                    n = LAY["fwdW", bp * Q + q]
                    bk.full(n)
                    for dst, src in forth_from_w(n, q):
                        last = nc.vector.tensor_copy(dst, src)
                    last.then_inc(drained[n % BANKS], 1)

                for c in range(NCH):
                    n = LAY["conv2", c]
                    bk.full(n)
                    xc = rows(X0, REG, c // Q, CH * (c % Q), CH)
                    nc.vector.scalar_tensor_tensor(xc, in0=by_row(bank(n)), scalar=STEP, in1=xc, op0=ALU.mult,
                                                   op1=ALU.add).then_inc(drained[n % BANKS], 1)
                    bk.result(n)
                    ins = nc.vector.bn_stats(stats[:, 6 * c:6 * c + 6], xc)
                    if c == FWDW_AT:
                        for q in range(0, Q, 2):
                            keep_fwdW(0, q)
                link(ins)
                aggregate()
                for k in range(1, BP + 4):
                    if 0 <= k - 2 < BP:
                        n = LAY["slot0", k - 2]
                        bk.full(n)
                        t0 = tabT[:, :].rearrange("p (c s) -> p c s", s=SL)[:, :, 0:1].broadcast_to([128, C, 2])
                        nc.vector.tensor_tensor(slot0.rearrange("p (c b) -> p c b", b=2),
                                                bank(n)[:, 0:2 * C].rearrange("p (c b) -> p c b", b=2), t0, op=ALU.mult)\
                            .then_inc(drained[n % BANKS], 1)
                    for q in range(Q):
                        if 0 <= k - 2 < BP:
                            n = LAY["fwdH", (k - 2) * Q + q]
                            bk.full(n)
                            src = bank(n)[:, 0:16 * (SL - 1)].rearrange("p (c b s) -> p c b s", c=8, b=2)
                            tt = tabT[:, 8 * SL * q:8 * SL * (q + 1)].rearrange("p (c s) -> p c s", s=SL)[:, :, 1:SL]\
                                .unsqueeze(2).broadcast_to([128, 8, 2, SL - 1])
                            to = spec[:, N * q:N * q + N].rearrange("p (c b s) -> p c b s", c=8, b=2)[:, :, :, 1:SL]
                            nc.vector.tensor_tensor(to, src, tt, op=ALU.mult).then_inc(drained[n % BANKS], 1)
                    if k == 2:
                        spread_of_means(2)
                    for q in range(0, Q, 2 if k - 1 < SHARED else 1):
                        if 1 <= k - 1 < BP:
                            keep_fwdW(k - 1, q)
                    for q in range(1, Q, 2):
                        if k - 3 == BP - 1:
                            n = LAY["invH", (k - 3) * Q + q]
                            bk.full(n)
                            for dst, src in back_from_h(n, k - 3, q):
                                last = nc.vector.tensor_copy(dst, src)
                            last.then_inc(drained[n % BANKS], 1)
                    if k == 2:
                        variance(2)
                    if k == 3:
                        scale_and_bias(2)
                        if not last_layer:
                            prepare(j + 1)
                            prepare_taps(j + 1)

            assert count[0] == PRO_LINKS, count
            with dve.Fori(0, DEPTH - 1) as j:
                layer(j)
                assert count[0] == LAY_LINKS, count
            layer(DEPTH - 1, last_layer=True)

        @block.tensor
        def _(pe):
            def conv(bk, n, c, X, X2_, weights, form_stride):
                bp, q = divmod(c, Q)
                bk.claim(n)
                out_b = bank(n)
                for dj in range(3):
                    for r in range(R):
                        form, src, g = ((1, X2_, CH * q), (0, X, CH * q), (1, X, CH * q), (0, X2_, CH * q + 1))[r]
                        reg = REG2 if r in (0, 3) else REG
                        o = form * form_stride + dj * C
                        last = nc.tensor.matmul(out_b[C * r:C * r + C, :], weights[:, o:o + C],
                                                rows(src, reg, bp, g, CH, dj - 1), start=(dj == 0), stop=(dj == 2),
                                                tile_position=(0, C * r))
                last.then_inc(filled[n % BANKS], 1)

            bk = Bank(pe, 0)
            pe.wait_ge(consts_in, 16 * 6)
            pe.wait_ge(zeroed, 1)

            def hidden_conv(c, shifts=range(3)):
                bp, q = divmod(c, Q)
                n = PRO["conv", c]
                if shifts[0] == 0:
                    if q == 0:
                        pe.wait_ge(x2_in[bp], 32)
                    bk.claim(n)
                for dj in shifts:
                    for t, (src, reg, g) in enumerate(((X2, REG2, CH * q), (X0, REG, CH * q), (X2, REG2, CH * q + 1))):
                        o = (3 * t + dj) * C
                        last = nc.tensor.matmul(bank(n)[C * t:C * t + C, :], w1S[:, o:o + C], rows(src, reg, bp, g, CH, dj - 1),
                                                start=(dj == 0), stop=(dj == 2), tile_position=(0, C * t))
                if shifts[-1] == 2:
                    last.then_inc(filled[n % BANKS], 1)

            def logits(h):
                n = PRO["logits", h]
                bk.claim(n)
                pe.wait_ge(hid_ready, 2 * h + 2)
                for g in range(8):
                    p = (8 * (h % 2) + g) * 128
                    last = nc.tensor.matmul(bank(n)[:, 36 * g:36 * g + 36], hid[0:3 * C, p:p + 128], w2S[:, :],
                                            start=True, stop=True)
                last.then_inc(filled[n % BANKS], 1)

            def turn_probs(c):
                n = PRO["probsT", c]
                bk.claim(n)
                pe.wait_ge(parts_cut, 3 * (c // 2) + 3)
                for g in range(CH):
                    p = (CH * (c % Q) + g) * 108
                    last = nc.tensor.transpose(bank(n).bitcast(bf16)[0:108, 128 * g:128 * g + 128], p3[:, p:p + 108],
                                               idbS[:, :])
                last.then_inc(filled[n % BANKS], 1)

            def add_up(c, i):
                n = PRO["sum", c]
                if i == 0:
                    bk.claim(n)
                bk.result(PRO["spread", c, pe_taps(c)[i]])
                last = nc.tensor.matmul(bank(n), cm(C_ID), pe_product(c, i), start=(i == 0),
                                        stop=(i == len(pe_taps(c)) - 1))
                if i == len(pe_taps(c)) - 1:
                    last.then_inc(filled[n % BANKS], 1)

            def spread(c, k):
                n = PRO["spread", c, k]
                bk.claim(n)
                bk.result(PRO["probsT", c])
                nc.tensor.matmul(bank(n), selS[:, 128 * k:128 * k + 128], pT[0:108, N * (c % Q):N * (c % Q) + N],
                                 start=True, stop=True).then_inc(filled[n % BANKS], 1)

            for c in range(Q):
                hidden_conv(c)
                if c % 2:
                    logits(c // 2)
            turn_probs(0)
            turn_probs(1)
            for c in range(NCH):
                for what, *args in prologue_chunk(c):
                    if what == "spread":
                        spread(*args)
                    elif what == "conv":
                        hidden_conv(args[0], range(args[1], args[1] + 1))
                    elif what == "sum":
                        add_up(*args)
                    elif what == "probsT":
                        turn_probs(*args)
                    else:
                        logits(*args)
            for i in range(len(pe_taps(NCH - 1))):
                add_up(NCH - 1, i)

            def layer(j):
                bk = Bank(pe, PRO_ROUNDS + LAY_ROUNDS * j)
                pe.wait_ge(weights_ready, j + 1)
                for c in range(NCH):
                    if c % Q == 0:
                        pe.wait_ge(x2_in[c // Q], 32 * (j + 2))
                    conv(bk, LAY["conv1", c], c, X0, X2, wts, 3 * C)

                def table(i):
                    n = LAY["table", i]
                    bk.claim(n)
                    e = (C_ERE, C_EIM)[i // 2]
                    nc.tensor.matmul(bank(n), cm(e, k=12), taps[:, N * (i % 2):N * (i % 2) + N], start=True,
                                     stop=True).then_inc(filled[n % BANKS], 1)

                def average(what, which, sem_, col):
                    n = LAY[what, which]
                    bk.claim(n)
                    pe.wait_ge(sem_, 2 * j + which)
                    nc.tensor.matmul(bank(n)[:, 0:1], cm(C_AVG), small[:, col:col + 1], start=True,
                                     stop=True).then_inc(filled[n % BANKS], 1)

                pe.wait_ge(prep_done, j + 1)
                table(0)
                average("mean", 1, mean_in, 0)
                table(1)
                average("var", 1, var_in, 4)
                table(2)
                table(3)

                def turn(bp, q):
                    c = bp * Q + q
                    n = LAY["turn", c]
                    bk.claim(n)
                    made(bk, LAY["conv2", c], n)
                    for g in range(CH):
                        last = nc.tensor.transpose(bank(n)[:, 128 * g:128 * g + 128],
                                                   rows(X0, REG, bp, CH * q + g, 1)[:, 0], cm(C_ID))
                    last.then_inc(filled[n % BANKS], 1)

                def forward_w(bp, q):
                    n = LAY["fwdW", bp * Q + q]
                    bk.claim(n)
                    for i in range(Q if q == 0 else 0):
                        made(bk, LAY["turn", bp * Q + i], n)
                    for i in range(4):
                        p = (4 * q + i) * 128
                        last = nc.tensor.matmul(bank(n)[:, 128 * i:128 * i + 128], turned[:, p:p + 128],
                                                cm(C_FW), start=True, stop=True)
                    last.then_inc(filled[n % BANKS], 1)

                def inverse_h(bp, q):
                    c = bp * Q + q
                    n, slot_0 = LAY["invH", c], LAY["slot0c", bp]
                    bk.claim(n)
                    made(bk, LAY["fwdH", c], slot_0, n)
                    made(bk, slot_0, n)
                    for cp in range(4):
                        p = N * q + 128 * cp
                        last = nc.tensor.matmul(bank(n)[:, 128 * cp:128 * cp + 128], spec[:, p:p + 128], cm(C_IH),
                                                start=True, stop=True)
                    last.then_inc(filled[n % BANKS], 1)

                def inverse_w(bp, q):
                    n = LAY["invW", bp * Q + q]
                    bk.claim(n)
                    for i in range(Q if q == 0 else 0):
                        made(bk, LAY["invH", bp * Q + i], n)
                    for g in range(CH):
                        p = (CH * q + g) * 128
                        last = nc.tensor.matmul(bank(n)[:, 128 * g:128 * g + 128], backw[bp % 2][:, p:p + 128], cm(C_IW),
                                                start=True, stop=True)
                    last.then_inc(filled[n % BANKS], 1)

                pe.wait_ge(edges, 1)
                for c in range(NCH):
                    if c % Q == 0:
                        pe.wait_ge(relu_done, 2 * BP * j + 2 * (c // Q) + 1)
                    if c % Q == 1:
                        pe.wait_ge(relu_done, 2 * BP * j + 2 * (c // Q) + 2)
                    conv(bk, LAY["conv2", c], c, Z0, Z2, wts[:, 2 * 3 * C:], 3 * C)
                    for q in range(Q):
                        if c == TURN_AT:
                            turn(0, q)
                        if c == FWDW_AT:
                            forward_w(0, q)
                for k in range(1, BP + 4):
                    for stage, lag in inverse_stages(k):
                        for q in range(Q):
                            if 0 <= k - lag < BP:
                                (inverse_w if stage == "invW" else inverse_h)(k - lag, q)
                    if 0 <= k - 2 < BP:
                        n = LAY["slot0", k - 2]
                        bk.claim(n)
                        for q in range(Q):
                            made(bk, LAY["fwdW", (k - 2) * Q + q], n)
                        nc.tensor.matmul(bank(n)[:, 0:2 * C], cm(C_HH), freqw[:, :].rearrange("p (a s) -> p a s", s=SL)[:, :, 0],
                                         start=True, stop=True).then_inc(filled[n % BANKS], 1)
                    for q in range(Q):
                        if 0 <= k - 2 < BP:
                            c = (k - 2) * Q + q
                            n = LAY["fwdH", c]
                            bk.claim(n)
                            nc.tensor.matmul(bank(n)[:, 0:16 * (SL - 1)], cm(C_FH),
                                             freqw[:, N * q:N * q + N].rearrange("p (a s) -> p a s", s=SL)[:, :, 1:SL],
                                             start=True, stop=True).then_inc(filled[n % BANKS], 1)
                    if k == 2:
                        average("mean", 2, mean_in, 0)
                    for q in range(Q):
                        if 1 <= k - 1 < BP:
                            forward_w(k - 1, q)
                    if 0 <= k - 2 < BP:
                        n = LAY["slot0c", k - 2]
                        bk.claim(n)
                        made(bk, LAY["slot0", k - 2], n)
                        nc.tensor.matmul(bank(n)[:, 0:2 * C], cm(C_HC), slot0, start=True, stop=True)\
                            .then_inc(filled[n % BANKS], 1)
                    for q in range(Q):
                        if 0 <= k < BP:
                            turn(k, q)
                    if k == 2:
                        average("var", 2, var_in, 4)

            with pe.Fori(0, DEPTH - 1) as j:
                layer(j)
            layer(DEPTH - 1)


def constants():
    n = np.arange(64)
    th = 2 * np.pi / 64
    k = np.arange(SL)
    cos, sin = np.cos(th * np.outer(n, k)) / 8, np.sin(th * np.outer(n, k)) / 8
    alternating = np.cos(np.pi * n) / 8
    c = np.zeros((128, C_ALL), np.float64)
    c[:, C_ID:C_ID + 128] = np.eye(128)
    fw = np.stack([cos, -sin], 1)
    fw[:, 1, 0] = alternating
    c[:, C_FW:C_FW + 128] = np.einsum("wts,bd->wbdts", fw, np.eye(2)).reshape(128, 128)
    iw = np.stack([2 * cos, -2 * sin], 1)
    iw[:, 0, 0], iw[:, 1, 0] = 1 / 8, alternating
    c[:, C_IW:C_IW + 128] = np.einsum("wts,bd->tbswd", iw, np.eye(2)).reshape(128, 128)
    cos, sin = np.cos(th * np.outer(n, n)) / 8, np.sin(th * np.outer(n, n)) / 8
    complex_h = np.block([[cos, -sin], [sin, cos]])
    hartley_h = np.kron(np.eye(2), cos + sin)
    c[:, C_FH:C_FH + 128] = complex_h
    c[:, C_IH:C_IH + 128] = complex_h.T
    c[:, C_HH:C_HH + 128] = hartley_h
    c[:, C_HC:C_HC + 128] = np.round(hartley_h @ complex_h, 6)
    c[:, C_AVG:C_AVG + 128] = np.kron(np.ones((R, R)), np.eye(C)) / R
    for part in range(2):
        freq = np.where(k > 0, k, 32 * part)
        for i in range(3):
            q = part * 6 + i * 2
            a = th * n * (i - 1)
            s = slice(64 * part, 64 * part + 64)
            c[q, C_ERE:C_ERE + 128][s], c[q + 1, C_ERE:C_ERE + 128][s] = np.cos(a), -np.sin(a)
            c[q, C_EIM:C_EIM + 128][s], c[q + 1, C_EIM:C_EIM + 128][s] = np.sin(a), np.cos(a)
            c[q, C_CS:C_CS + SL], c[q + 1, C_CS:C_CS + SL] = np.cos(th * freq), np.sin(th * freq)
            c[q, C_ONE] = 1
            c[q, C_SGN], c[q + 1, C_SGN] = 1, -1
    for form in range(2):
        c[C * form:C * (form + 3), C_MASK + form] = -1.0 / TAPS
    sel = np.zeros((3, R, TAPS, TAPS, R, C), np.float32)
    for r in range(R):
        for k in range(TAPS):
            sel[:, r, k, k, r, :] = 1
    return c.astype(np.float32), sel.reshape(3 * R * TAPS, TAPS * 128), np.eye(128, dtype=np.float32)


def windows(k):
    o = np.zeros((R, k.shape[1], 2, 3, k.shape[3]), np.float32)
    for form in range(2):
        for di in range(3):
            o[di + form, :, form] = k[di]
    return o.reshape(128, -1)


def kernel(x, L0_conv_w1, L0_conv_b1, L0_conv_w2, L0_conv_b2, L1_conv_K, L1_conv_L, L1_conv_gamma, L1_conv_beta):
    import ml_dtypes
    import concourse.bacc as bacc
    from concourse.bass_utils import run_bass_kernel_spmd

    x, w1, b1, w2, b2, K, L, gamma, beta = (np.asarray(a) for a in (
        x, L0_conv_w1, L0_conv_b1, L0_conv_w2, L0_conv_b2, L1_conv_K, L1_conv_L, L1_conv_gamma, L1_conv_beta))
    cst, sel, idb = constants()
    par = np.zeros((DEPTH, 128, P_ALL), np.float32)
    for j in range(DEPTH):
        for k, kern in enumerate((K[j].transpose(2, 1, 3, 0), K[j].transpose(2, 0, 3, 1)[::-1, :, ::-1])):
            flat = kern.transpose(1, 0, 2, 3).reshape(C, -1)
            for r in range(R):
                par[j, C * r:C * r + C, P_K + k * TAPS * C:P_K + (k + 1) * TAPS * C] = flat
            par[j, :, P_F + k * 6 * C:P_F + (k + 1) * 6 * C] = windows(kern)
        for r in range(R):
            par[j, C * r:C * r + C, P_GB] = gamma[j]
            par[j, C * r:C * r + C, P_GB + 1] = beta[j]
        for part in range(2):
            for i in range(3):
                for tr in range(2):
                    q = part * 6 + i * 2 + tr
                    par[j, q, P_L:P_L9] = L[j, :, 0, i, :].reshape(-1)
                    par[j, q, P_L9:P_ALL] = L[j, :, 0].reshape(-1)
    w1f = windows(w1.transpose(2, 1, 3, 0)).reshape(128, 2, 3, HID)
    w1p = np.zeros((128, 3, 3, C), np.float32)
    b1p = np.zeros((3, C, 1), np.float32)
    w2p = np.zeros((3, C, R, TAPS), np.float32)
    for r, (tile, slot, form) in enumerate(((0, 0, 1), (1, 0, 0), (1, HID, 1), (2, 0, 0))):
        w1p[:, tile, :, slot:slot + HID] = w1f[:, form]
        b1p[tile, slot:slot + HID, 0] = b1
        w2p[tile, slot:slot + HID, r] = w2[:, :, 0, 0].T
    b1p[0, HID, 0] = 1.0
    w2p[0, HID, :] = b2
    arrays = {
        "x": x, "par": par, "w1": w1p.reshape(128, -1), "b1": b1p.reshape(3 * C, 1), "w2": w2p.reshape(3 * C, R * TAPS),
        "cst": cst, "sel": sel.astype(ml_dtypes.bfloat16), "idb": idb.astype(ml_dtypes.bfloat16),
    }
    nc = bacc.Bacc("TRN2", target_bir_lowering=False, num_devices=1)
    args = [nc.dram_tensor(n, a.shape, mybir.dt.from_np(a.dtype), kind="ExternalInput").ap() for n, a in arrays.items()]
    out = nc.dram_tensor("out", (B, C, H, W), mybir.dt.float32, kind="ExternalOutput").ap()
    build(nc, *args, out)
    r = run_bass_kernel_spmd(nc, [arrays], core_ids=[0])
    return r.results[0]["out"]
```
